# Optimizing a Trainium2 kernel written in Bass

```python
import numpy as np
import jax
import jax.numpy as jnp

def _softmax(x, axis=-1):
    return jax.nn.softmax(x, axis=axis)

def _gelu(x):
    return jax.nn.gelu(x, approximate=True)

def _silu(x):
    return jax.nn.silu(x)

def _sigmoid(x):
    return jax.nn.sigmoid(x)

def _layernorm(x, axis=-1, eps=1e-05):
    m = jnp.mean(x, axis=axis, keepdims=True)
    v = jnp.var(x, axis=axis, keepdims=True)
    return (x - m) / jnp.sqrt(v + eps)

def _scatter_add(tgt, idx, src, axis=0):
    return tgt.at[idx].add(src)

def _segment_sum(src, seg, n):
    return jax.ops.segment_sum(src, seg, n)
kernel_name = 'mk_prb_d1_jaxref_r8_49c55d'

def setup_inputs(seed: int=0):
    np.random.seed(seed)
    _w = jnp.asarray

    def _L0_attn_setup():
        import jax, jax.numpy as jnp
        import numpy as np
        D_MODEL = 256
        HEADS = 16
        HEAD_DIM = D_MODEL // HEADS
        key = jax.random.key(seed)
        k1, k2, k3 = jax.random.split(key, 3)
        B, S = (1, 256)
        x = jax.random.normal(k1, (B, S, D_MODEL), dtype=jnp.float32)
        Wqkv_w = jax.random.normal(k2, (D_MODEL + 2 * HEAD_DIM, D_MODEL), dtype=jnp.float32) * D_MODEL ** (-0.5)
        Wqkv_b = jnp.zeros((D_MODEL + 2 * HEAD_DIM,), dtype=jnp.float32)
        out_w = jax.random.normal(k3, (D_MODEL, D_MODEL), dtype=jnp.float32) * D_MODEL ** (-0.5)
        out_b = jnp.zeros((D_MODEL,), dtype=jnp.float32)
        return {'x': x, 'Wqkv_w': Wqkv_w, 'Wqkv_b': Wqkv_b, 'out_w': out_w, 'out_b': out_b}
    _L0_attn_in = _L0_attn_setup()

    def _L0_ffn_setup():
        import jax, jax.numpy as jnp
        import numpy as np
        D_MODEL = 256
        FFN_HIDDEN = 256
        N_EXPERTS = 16
        TOP_K = 4
        key = jax.random.key(seed)
        k1, k2, k3, k4, k5 = jax.random.split(key, 5)
        scale = 1.0 / np.sqrt(D_MODEL)
        x = jax.random.normal(k1, (2, 512, D_MODEL), dtype=jnp.float32)
        w_router = jax.random.normal(k2, (N_EXPERTS, D_MODEL), dtype=jnp.float32) * scale
        w_gate = jax.random.normal(k3, (N_EXPERTS, D_MODEL, FFN_HIDDEN), dtype=jnp.float32) * scale
        w_up = jax.random.normal(k4, (N_EXPERTS, D_MODEL, FFN_HIDDEN), dtype=jnp.float32) * scale
        w_down = jax.random.normal(k5, (N_EXPERTS, FFN_HIDDEN, D_MODEL), dtype=jnp.float32) * (1.0 / np.sqrt(FFN_HIDDEN))
        return {'x': x, 'w_router': w_router, 'w_gate': w_gate, 'w_up': w_up, 'w_down': w_down}
    _L0_ffn_in = _L0_ffn_setup()
    _d = {'L0_attn_x': _L0_attn_in['x'], 'L0_attn_Wqkv_w': _L0_attn_in['Wqkv_w'], 'L0_attn_Wqkv_b': _L0_attn_in['Wqkv_b'], 'L0_attn_out_w': _L0_attn_in['out_w'], 'L0_attn_out_b': _L0_attn_in['out_b'], 'L0_ffn_w_router': _L0_ffn_in['w_router'], 'L0_ffn_w_gate': _L0_ffn_in['w_gate'], 'L0_ffn_w_up': _L0_ffn_in['w_up'], 'L0_ffn_w_down': _L0_ffn_in['w_down']}
    _x0 = _d['L0_attn_x']
    _d['L0_attn_x'] = jax.random.normal(jax.random.fold_in(jax.random.key(seed), 1), (8, 256, 256), dtype=_x0.dtype)
    del _x0
    return _d

def reference(L0_attn_x, L0_attn_Wqkv_w, L0_attn_Wqkv_b, L0_attn_out_w, L0_attn_out_b, L0_ffn_w_router, L0_ffn_w_gate, L0_ffn_w_up, L0_ffn_w_down):

    def _L0_attn_ref(x, Wqkv_w, Wqkv_b, out_w, out_b):
        import jax, jax.numpy as jnp
        import numpy as np
        D_MODEL = 256
        HEADS = 16
        HEAD_DIM = D_MODEL // HEADS
        B, S, _ = x.shape
        qkv = jnp.einsum('bsd,ed->bse', x, Wqkv_w) + Wqkv_b
        q = qkv[..., :D_MODEL]
        k = qkv[..., D_MODEL:D_MODEL + HEAD_DIM]
        v = qkv[..., D_MODEL + HEAD_DIM:]
        q = q.reshape(B, S, HEADS, HEAD_DIM)
        scale = 1.0 / np.sqrt(HEAD_DIM)
        scores = jnp.einsum('bqhd,bkd->bhqk', q, k) * scale
        min_val = jnp.finfo(scores.dtype).min
        causal = jnp.tril(jnp.ones((S, S), dtype=bool))
        scores = jnp.where(causal[None, None], scores, min_val)
        attn = jax.nn.softmax(scores, axis=-1)
        ctx = jnp.einsum('bhqk,bkd->bqhd', attn, v)
        ctx = ctx.reshape(B, S, D_MODEL)
        out = jnp.einsum('bsd,ed->bse', ctx, out_w) + out_b
        return out

    def _L0_ffn_ref(x, w_router, w_gate, w_up, w_down):
        import jax, jax.numpy as jnp
        import numpy as np
        D_MODEL = 256
        FFN_HIDDEN = 256
        N_EXPERTS = 16
        TOP_K = 4
        B, S, D = x.shape
        xt = x.reshape(-1, D)
        logits = jnp.einsum('td,ed->te', xt, w_router)
        probs = jax.nn.softmax(logits, axis=-1)
        top_w, top_e = jax.lax.top_k(probs, TOP_K)
        top_w = top_w / jnp.sum(jnp.abs(top_w), axis=-1, keepdims=True)
        out = jnp.zeros_like(xt)
        for e in range(N_EXPERTS):
            coeff = jnp.sum(jnp.where(top_e == e, top_w, 0.0), axis=-1)
            h = jax.nn.silu(xt @ w_gate[e]) * (xt @ w_up[e])
            out = out + coeff[:, None] * (h @ w_down[e])
        return out.reshape(B, S, D)
    x = L0_attn_x
    xn = _layernorm(x, axis=-1)
    x = x + _L0_attn_ref(xn, L0_attn_Wqkv_w, L0_attn_Wqkv_b, L0_attn_out_w, L0_attn_out_b) + _L0_ffn_ref(xn, L0_ffn_w_router, L0_ffn_w_gate, L0_ffn_w_up, L0_ffn_w_down)
    return x

_drawn_inputs = setup_inputs


def setup_inputs(seed=0):
    import zlib

    import numpy as np

    out = dict(_drawn_inputs(seed))
    spreads = {'L0_attn_Wqkv_b': (0.0, 0.1), 'L0_attn_out_b': (0.0, 0.1)}
    factors = {}
    for name, (base, spread) in spreads.items():
        noise = np.random.default_rng([zlib.crc32(name.encode()), seed]).standard_normal(out[name].shape)
        drawn = base * np.exp(spread * noise) if base else spread * noise
        out[name] = jnp.asarray(drawn.astype(out[name].dtype))
    for name, factor in factors.items():
        out[name] = (out[name] * factor).astype(out[name].dtype)
    return out
```

```python
from contextlib import ExitStack

import concourse.bass as bass
from concourse import mybir

ALU = mybir.AluOpType
ACT = mybir.ActivationFunctionType
AX = mybir.AxisListType
F32 = mybir.dt.float32
F32R = mybir.dt.float32r
BF16 = mybir.dt.bfloat16
I32 = mybir.dt.int32
U32 = mybir.dt.uint32

P = 128
TOP_K = 4
LN_EPS = 1e-5
MASKED = -1e30


class Steps:

    def __init__(self, eng, sem):
        self.eng, self.sem, self.n = eng, sem, 0

    def __call__(self, ins):
        self.n += 1
        ins.then_inc(self.sem, 1)
        self.eng.wait_ge(self.sem, self.n)


def attention_and_experts(nc, x, wqkv, bqkv, wout, bout, wrouter, wgate, wup, wdown, out):
    B, S, D = x.shape
    E, _, F = wgate.shape
    T = B * S
    NT = T // P
    HD = (wqkv.shape[0] - D) // 2
    H = D // HD
    KC = D // P
    FC = F // P
    GT = 4
    NG = NT // GT
    GW = GT * P
    NQ = H // 4
    RING = 4
    MT = -(-((T * TOP_K + E * (P - 1)) // P) // RING) * RING
    NOROW = T * TOP_K
    assert (D, S, F, HD, E, KC, FC) == (2 * P, 2 * P, 2 * P, 16, 16, 2, 2) and T & (T - 1) == 0
    VW = 32
    QSCALE = float(HD) ** -0.5

    x_rows = x.rearrange("b s d -> (b s) d")
    out_rows = out.rearrange("b s d -> (b s) d")

    xn_d = nc.dram_tensor("xn_d", (T, D), F32).ap()
    q_d = nc.dram_tensor("q_d", (2, D, T), F32).ap()
    k_d = nc.dram_tensor("k_d", (2, HD, T), F32).ap()
    slots_d = nc.dram_tensor("slots_d", (P * MT, 1), I32).ap()
    y_d = nc.dram_tensor("y_d", (TOP_K * T, D), F32).ap()

    with ExitStack() as ctx:
        def sb(name, shape, dt=F32):
            return ctx.enter_context(nc.sbuf_tensor(name, shape, dt))

        def sem(name):
            return ctx.enter_context(nc.semaphore(name))

        bank = ctx.enter_context(nc.psum_tensor("bank", [P, 8, 512], F32))

        wgu = sb("wgu", [P, E * KC, 2 * F])
        wdn = sb("wdn", [P, E * FC, D])
        xs = sb("xs", [P, NT, D])
        k_all = sb("k_all", [P, T], F32R)
        ks = sb("ks", [P, 2, S], F32R)
        v_all = sb("v_all", [P, NT, VW])
        vs = sb("vs", [P, 2, 2, VW])
        pt = sb("pt", [P, 6, 512])
        ct = sb("ct", [P, 2, NQ, S])
        ctx_n = sb("ctx_n", [P, D])
        cxt = sb("cxt", [P, KC, P])
        rden = sb("rden", [P, 2, H])
        nmax = sb("nmax", [P, 2, 2, H])
        mt = sb("mt", [H, 2, 2, S], F32R)
        ident = sb("ident", [P, P])
        ident_b = sb("ident_b", [P, P], BF16)
        below = sb("below", [P, P], BF16)
        ones_b = sb("ones_b", [P, P], BF16)
        mask_q = sb("mask_q", [P, 2, P], BF16)
        mask_k = sb("mask_k", [P, 4, P], BF16)
        wqT = sb("wqT", [P, KC, D])
        wvrkT = sb("wvrkT", [P, KC, 48])
        woT = sb("woT", [P, KC, D])
        bq = sb("bq", [P, KC])
        bq_s = sb("bq_s", [P, KC])
        bvrk = sb("bvrk", [48, 1])
        bo = sb("bo", [P, D])
        stats = sb("stats", [P, NT, 6])
        mv = sb("mv", [P, NT, 2])
        var_e = sb("var_e", [P, NT])
        std0 = sb("std0", [P, NT])
        rstd = sb("rstd", [P, NT])
        logits = sb("logits", [P, NT, E])
        probs = sb("probs", [P, NT, E])
        rowstat = sb("rowstat", [P, NT])
        top_w = sb("top_w", [P, NT, 8])
        top_e = sb("top_e", [P, NT, 8], U32)
        top_ef = sb("top_ef", [P, NT, TOP_K])
        coef = sb("coef", [P, NT, TOP_K])
        iota_e = sb("iota_e", [P, E])
        onehot = pt[:, 0:2, :].rearrange("p a n -> p (a n)").rearrange("p (t k e) -> p t k e", t=NT, k=TOP_K)
        chosen = sb("chosen", [P, NT, E], BF16)
        PADT = NT // 2
        scan_t = sb("scan_t", [P, 2, PADT + NT, E])
        PADE = E // 2
        scan_e = sb("scan_e", [P, 2, PADE + E])
        ntile_i = sb("ntile_i", [P, E], I32)
        first_row = sb("first_row", [P, E])
        slot_i = sb("slot_i", [P, NT, TOP_K], I32)
        slot_p = sb("slot_p", [P, NT, TOP_K], I32)
        slot_f = sb("slot_f", [P, NT, TOP_K])
        slot_pf = sb("slot_pf", [P, NT, TOP_K])
        row_of = sb("row_of", [P, NT, TOP_K], I32)
        tile_no = sb("tile_no", [1, MT])
        tile_ge = pt[0:1, 2:5, :].rearrange("p a n -> p (a n)")[:, 0:MT * E].rearrange("p (j e) -> p j e", j=MT)
        tile_ef = sb("tile_ef", [1, MT])
        tile_e = sb("tile_e", [1, MT], I32)
        scat_to = sb("scat_to", [P, 2, TOP_K], I32)
        scat_val = sb("scat_val", [P, 2, TOP_K], I32)
        put_row = sb("put_row", [P, MT + RING], I32)
        get_row = sb("get_row", [P, MT + RING], I32)
        get_now = sb("get_now", [P, RING], I32)
        put_now = sb("put_now", [P, RING], I32)

        WORK = 32 * 256
        with nc.sbuf_tensor("early", [P, WORK], F32) as early:
            pass
        with nc.sbuf_tensor("qs", [P, 2, H, S], F32R) as qs:
            pass
        late = sb("late", [P, WORK])

        def carve(region, spans, at=0):
            found = []
            for n in spans:
                found.append(region[:, at:at + n])
                at += n
            assert at <= WORK
            return found

        v_xn, v_xnT, v_qhl, v_khl, v_vr = carve(
            early, [2 * GT * D, 2 * KC * GW, 2 * KC * GW, 2 * GW, GW])
        xn = v_xn.rearrange("p (b u d) -> p b u d", b=2, u=GT)
        xnT = v_xnT.rearrange("p (b c t) -> p b c t", b=2, c=KC)
        qhl = v_qhl.bitcast(F32R).rearrange("p (a m t) -> p a m t", a=2, m=KC)
        khl = v_khl.bitcast(F32R).rearrange("p (a t) -> p a t", a=2)
        vr = v_vr
        v_wn, = carve(early, [KC * D + D + KC * D], at=2 * GT * D + 2 * KC * GW)
        wq_nat = v_wn[:, 0:KC * D].rearrange("p (m d) -> p m d", m=KC)
        wvrk_nat = v_wn[:, KC * D:KC * D + D]
        wo_nat = v_wn[:, KC * D + D:].rearrange("p (m d) -> p m d", m=KC)
        v_xg, v_xT, v_s, v_h, v_hT, v_y, v_yc, v_oc = carve(
            late, [RING * D, 2 * D, 2 * F, 2 * F, 2 * F, RING * D, 2 * TOP_K * D, 2 * D])
        xg = v_xg.rearrange("p (r d) -> p r d", r=RING)
        xT = v_xT.rearrange("p (b c t) -> p b c t", b=2, c=KC)
        sg = v_s.rearrange("p (b f) -> p b f", b=2)
        hh = v_h.rearrange("p (b f) -> p b f", b=2)
        hT = v_hT.rearrange("p (b c t) -> p b c t", b=2, c=FC)
        ys = v_y.rearrange("p (r d) -> p r d", r=RING)
        yc = v_yc.rearrange("p (b k d) -> p b k d", b=2, k=TOP_K)
        oc = v_oc.rearrange("p (b d) -> p b d", b=2)

        x_in = [sem(f"x_in{g}") for g in range(NG)]
        w_in = sem("w_in")
        experts_in = sem("experts_in")
        masks = sem("masks")
        consts = sem("consts")
        w_ps = sem("w_ps")
        w_act = sem("w_act")
        w_dve = sem("w_dve")
        var_ready = sem("var_ready")
        std_ready = sem("std_ready")
        dve_ln = sem("dve_ln")
        xn_ready = sem("xn_ready")
        xb_ready = sem("xb_ready")
        xn_stored = [sem(f"xn_stored{b}") for b in range(2)]
        xT_ps = sem("xT_ps")
        xT_act = sem("xT_act")
        xT_dve = sem("xT_dve")
        proj_ps = sem("proj_ps")
        vr_ready = sem("vr_ready")
        kh_ready = sem("kh_ready")
        kl_ready = sem("kl_ready")
        qh_ready = sem("qh_ready")
        ql_ready = sem("ql_ready")
        q_stored = sem("q_stored")
        k_stored = sem("k_stored")
        vrT_ps = sem("vrT_ps")
        vl_ready = sem("vl_ready")
        k_all_in = sem("k_all_in")
        dve_rt = sem("dve_rt")
        shifted = sem("shifted")
        exped = sem("exped")
        chosen_ready = sem("chosen_ready")
        place_ps = sem("place_ps")
        route_ready = sem("route_ready")
        tile_e_ready = sem("tile_e_ready")
        list_init = sem("list_init")
        init_stored = sem("init_stored")
        scat_copied = sem("scat_copied")
        scattered = [sem(f"scattered{b}") for b in range(2)]
        list_in = sem("list_in")
        rows_ready = sem("rows_ready")
        q_in = [[sem(f"q_in{b}{h}") for h in range(2)] for b in range(2)]
        kv_ready = sem("kv_ready")
        qs_padded = sem("qs_padded")
        p1_ps = sem("p1_ps")
        max_done = sem("max_done")
        mt_ps = sem("mt_ps")
        mth_ready = sem("mth_ready")
        mtl_ready = sem("mtl_ready")
        m_in = [sem(f"m_in{b}") for b in range(2)]
        s_ps = sem("s_ps")
        exp_done = sem("exp_done")
        pv_ps = sem("pv_ps")
        ct_ready = sem("ct_ready")
        c_ps = sem("c_ps")
        rden_ready = sem("rden_ready")
        ctx_ready = sem("ctx_ready")
        t_ps = sem("t_ps")
        cxt_ready = sem("cxt_ready")
        o_ps = sem("o_ps")
        o_added = sem("o_added")
        now_ready = sem("now_ready")
        pool_gate = sem("pool_gate")
        put_ready = sem("put_ready")
        gathered = [sem(f"gathered{r}") for r in range(RING)]
        y_sent = [sem(f"y_sent{r}") for r in range(RING)]
        xgT_ps = sem("xgT_ps")
        xgT_ready = sem("xgT_ready")
        gu_ps = sem("gu_ps")
        silu_ready = sem("silu_ready")
        h_ready = sem("h_ready")
        hT_ps = sem("hT_ps")
        hT_ready = sem("hT_ready")
        dn_ps = sem("dn_ps")
        y_ready = sem("y_ready")
        y_in = [sem(f"y_in{b}") for b in range(2)]
        combined = sem("combined")
        added = sem("added")
        out_sent = [sem(f"out_sent{b}") for b in range(2)]

        N_W = 10
        N_EXP = 12

        block = ctx.enter_context(nc.Block())

        @block.sync
        def _(sp):
            for g in range(NG):
                sp.dma_start(xs[:, g * GT:(g + 1) * GT, :],
                             x_rows[g * GW:(g + 1) * GW, :].rearrange("(u p) d -> p u d", p=P)
                             ).then_inc(x_in[g], 16)
            sp.dma_start(wq_nat, wqkv[0:D, :].rearrange("(m p) d -> p m d", p=P)).then_inc(w_in, 16)
            sp.dma_start(wvrk_nat[0:16, :], wqkv[D + HD:D + 2 * HD, :]).then_inc(w_in, 16)
            sp.dma_start(wvrk_nat[16:32, :], wrouter).then_inc(w_in, 16)
            sp.dma_start(wvrk_nat[32:48, :], wqkv[D:D + HD, :]).then_inc(w_in, 16)
            sp.dma_start(wo_nat, wout.rearrange("(m p) d -> p m d", p=P)).then_inc(w_in, 16)
            for m in range(KC):
                sp.dma_start(bq[:, m:m + 1], bqkv[m * P:(m + 1) * P].rearrange("(p a) -> p a", a=1)).then_inc(w_in, 16)
            sp.dma_start(bo[:, :], bout.partition_broadcast(P)).then_inc(w_in, 16)
            sp.wait_ge(consts, 1)
            sp.dma_start(bvrk[0:16, :], bqkv[D + HD:D + 2 * HD].rearrange("(p a) -> p a", a=1)).then_inc(w_in, 16)
            sp.dma_start(bvrk[32:48, :], bqkv[D:D + HD].rearrange("(p a) -> p a", a=1)).then_inc(w_in, 16)

            for g in range(NG):
                cols = slice(g * GW, (g + 1) * GW)
                sp.wait_ge(xn_ready, GT * (g + 1))
                sp.dma_start(xn_d[cols, :].rearrange("(u p) d -> p u d", p=P), xn[:, g % 2]
                             ).then_inc(xn_stored[g % 2], 16)
                sp.wait_ge(kl_ready, g + 1)
                for a in range(2):
                    sp.dma_start(k_d[a, :, cols], khl[32:48, a, :].bitcast(F32)).then_inc(k_stored, 16)
                sp.wait_ge(ql_ready, KC * (g + 1))
                for a in range(2):
                    sp.dma_start(q_d[a, :, cols].rearrange("(m p) t -> p m t", p=P), qhl[:, a].bitcast(F32)
                                 ).then_inc(q_stored, 16)
            sp.wait_ge(list_init, 1)
            sp.dma_start(slots_d.rearrange("(p j) a -> p (j a)", p=P), put_row[:, 0:MT]).then_inc(init_stored, 16)

            sp.wait_ge(k_stored, 32 * NG)
            for r in range(4):
                sp.dma_start(k_all[16 * r:16 * r + 16, :].bitcast(F32), k_d[r // 2]).then_inc(k_all_in, 16)
            sp.wait_ge(q_stored, 32 * NG)
            sp.wait_ge(vrT_ps, NG)
            for r in range(2):
                sp.wait_ge(xn_stored[r], 16 * NG // 2)

            def load_q(b, buf, half):
                hs = slice(half * H // 2, (half + 1) * H // 2)
                for r in range(4):
                    src = q_d[r % 2].rearrange("(h d) t -> d h t", d=HD)[:, hs, bass.ds(b * S, S)]
                    sp.dma_start(qs[16 * r:16 * r + 16, buf, hs, :].bitcast(F32), src).then_inc(q_in[buf][half], 16)

            def load_m(b, buf):
                sp.wait_ge(mtl_ready, b + 1)
                for a in range(2):
                    sp.dma_start(qs[64 + a:65 + a, buf, :, :].bitcast(F32), mt[:, buf, a, :].bitcast(F32)).then_inc(m_in[buf], 16)

            def load_next(b, buf):
                sp.wait_ge(s_ps, 12 * (b - 2) + 6)
                load_q(b, buf, 0)
                sp.wait_ge(s_ps, 12 * (b - 2) + 12)
                load_q(b, buf, 1)

            for b in range(2):
                for half in range(2):
                    load_q(b, b, half)
            sp.wait_ge(qs_padded, 1)
            load_m(0, 0)
            load_m(1, 1)
            with sp.Fori(1, B // 2) as i:
                for u in range(2):
                    load_next(i * 2 + u, u)
                    load_m(i * 2 + u, u)

            for b in range(2):
                sp.wait_ge(scattered[b], 16 * TOP_K * NT // 2)
            sp.dma_start(put_row[:, 0:MT], slots_d.rearrange("(p j) a -> p (j a)", p=P)).then_inc(list_in, 16)

            for r in range(RING):
                sp.wait_ge(y_sent[r], 16 * (MT // RING))

            def load_y(t, buf):
                sp.dma_start(yc[:, buf], y_d.rearrange("(k t) d -> t k d", k=TOP_K)[bass.ds(t * P, P)]
                             ).then_inc(y_in[buf], 16)

            def store_out(t, buf):
                sp.wait_ge(added, t + 1)
                sp.dma_start(out_rows[bass.ds(t * P, P), :], oc[:, buf]).then_inc(out_sent[buf], 16)

            load_y(0, 0)
            load_y(1, 1)
            with sp.Fori(0, NT // 2 - 1) as i:
                for u in range(2):
                    store_out(i * 2 + u, u)
                    load_y(i * 2 + u + 2, u)
            for u in range(2):
                store_out(NT - 2 + u, u)
            for u in range(2):
                sp.wait_ge(out_sent[u], 16 * NT // 2)

        @block.gpsimd
        def _(pool):
            const = Steps(pool, masks)
            pool.memset(bvrk[:, :], 0.0).then_inc(consts, 1)
            pool.wait_ge(consts, 1)
            for t in (ident, ident_b):
                const(pool.memset(t[:, :], 0.0))
            for t in (ident, ident_b):
                const(pool.affine_select(out=t[:, :], in_=t[:, :], compare_op=ALU.not_equal, fill=1.0, base=0,
                                   pattern=[[-1, P]], channel_multiplier=1))
            const(pool.memset(mask_q[:], 0.0))
            const(pool.memset(mask_k[:], 0.0))
            const(pool.memset(below[:], 1.0))
            const(pool.affine_select(out=mask_q[:], in_=mask_q[:], compare_op=ALU.is_ge, fill=MASKED, base=0,
                               pattern=[[0, 2], [-1, P]], channel_multiplier=1))
            const(pool.affine_select(out=mask_k[:], in_=mask_k[:], compare_op=ALU.is_ge, fill=MASKED, base=0,
                               pattern=[[0, 4], [1, P]], channel_multiplier=-1))
            const(pool.affine_select(out=below[:], in_=below[:], compare_op=ALU.is_ge, fill=0.0, base=-1,
                               pattern=[[1, P]], channel_multiplier=-1))
            const(pool.memset(ones_b[:], 1.0))
            const(pool.memset(k_all[64:128].bitcast(F32), 0.0))
            const(pool.memset(ks[64:128].bitcast(F32), 0.0))
            const(pool.memset(v_all[:, :, HD + 1:VW], 0.0))
            const(pool.memset(v_all[:, :, HD:HD + 1], 1.0))
            const(pool.memset(ks[64:66].bitcast(F32), 1.0))
            const(pool.memset(scan_t[:], 0.0))
            const(pool.memset(scan_e[:], 0.0))
            const(pool.iota(iota_e[:], [[1, E]], base=0, channel_multiplier=0,
                      allow_small_or_imprecise_dtypes=True))
            const(pool.iota(row_of[:], [[P, NT], [T, TOP_K]], base=0, channel_multiplier=1))
            const(pool.iota(tile_no[:], [[1, MT]], base=0, channel_multiplier=0,
                      allow_small_or_imprecise_dtypes=True))
            pool.iota(put_row[:], [[0, MT + RING]], base=NOROW, channel_multiplier=0).then_inc(list_init, 1)

            pool.wait_ge(w_in, 16 * N_W)
            for t in range(NT):
                pool.wait_ge(xn_ready, t + 1)
                pool.tensor_tensor(xs[:, t, :], xs[:, t, :], bo[:, :], ALU.add).then_inc(xb_ready, 1)

            def copy_kv(b, buf):
                if not isinstance(b, int) or b:
                    pool.wait_ge(kv_ready, b * 2)
                pool.wait_ge(k_all_in, 64)
                pool.tensor_copy(ks[0:64, buf, :], k_all[0:64, bass.ds(b * S, S)]).then_inc(kv_ready, 1)
                pool.wait_ge(kv_ready, b * 2 + 1)
                pool.tensor_copy(vs[:, buf], v_all[:, bass.ds(b * 2, 2), :]).then_inc(kv_ready, 1)

            pool.wait_ge(vrT_ps, NG)
            pool.wait_ge(q_stored, 32 * NG)
            pool.wait_ge(k_stored, 32 * NG)
            for r in range(2):
                pool.wait_ge(xn_stored[r], 16 * NG // 2)
            pool.wait_ge(xb_ready, NT)
            pool.memset(qs[64:128].bitcast(F32), 0.0).then_inc(qs_padded, 1)
            pool.wait_ge(qs_padded, 1)
            pool.wait_ge(vl_ready, NG)
            copy_kv(0, 0)
            copy_kv(1, 1)

            pool.wait_ge(kv_ready, 4)
            pool.wait_ge(init_stored, 16)
            pool.wait_ge(route_ready, 1)
            last_slot = pool.to_reg(P * MT - 1)

            def copied(sem, value):
                pool.wait_ge(sem, value)
                pool.sem_inc(pool_gate, 1)

            def scatter_slots(t, buf, used):
                if used is not None:
                    pool.wait_ge(route_ready, 1)
                    pool.wait_ge(scattered[buf], used)
                pool.tensor_copy(scat_to[:, buf, :], slot_i[:, bass.ds(t, 1), :]).then_inc(scat_copied, 1)
                pool.tensor_copy(scat_val[:, buf, :], row_of[:, bass.ds(t, 1), :]).then_inc(scat_copied, 1)
                for k in range(TOP_K):
                    if k == 0:
                        copied(scat_copied, t * 2 + 2)
                    pool.indirect_dma_start(
                        slots_d, bass.IndirectOffsetOnAxis(ap=scat_to[:, buf, k:k + 1], axis=0),
                        scat_val[:, buf, k:k + 1], None, bounds_check=last_slot, oob_is_err=False,
                    ).then_inc(scattered[buf], 16)

            for u in range(2):
                scatter_slots(u, u, None)
            with pool.Fori(1, B) as b:
                for u in range(2):
                    scatter_slots(b * 2 + u, u, b * (16 * TOP_K))
            with pool.Fori(1, B // 2) as i:
                for u in range(2):
                    b = i * 2 + u
                    pool.wait_ge(k_all_in, 64)
                    pool.wait_ge(pv_ps, (b - 1) * NQ)
                    copy_kv(b, u)

            pool.wait_ge(kv_ready, 2 * B)
            pool.wait_ge(rows_ready, 1)
            last_row = pool.to_reg(T - 1)
            last_out = pool.to_reg(T * TOP_K - 1)
            pool.wait_ge(s_ps, 12 * B)

            def gather(j, r, wait):
                if wait:
                    pool.wait_ge(xgT_ps, j - RING + 1)
                pool.tensor_copy(get_now[:, r:r + 1], get_row[:, bass.ds(j, 1)]).then_inc(now_ready, 1)
                copied(now_ready, j + 1)
                pool.indirect_dma_start(
                    xg[:, r, :], None, xn_d, bass.IndirectOffsetOnAxis(ap=get_now[:, r:r + 1], axis=0),
                    bounds_check=last_row, oob_is_err=False).then_inc(gathered[r], 16)

            def send(j, r):
                pool.wait_ge(y_ready, j + 1)
                pool.tensor_copy(put_now[:, r:r + 1], put_row[:, bass.ds(j, 1)]).then_inc(put_ready, 1)
                copied(put_ready, j + 1)
                pool.indirect_dma_start(
                    y_d, bass.IndirectOffsetOnAxis(ap=put_now[:, r:r + 1], axis=0), ys[:, r, :], None,
                    bounds_check=last_out, oob_is_err=False).then_inc(y_sent[r], 16)

            AHEAD = RING - 1

            def tiles(base, first):
                for u in range(RING):
                    gather(base + u + AHEAD, (u + AHEAD) % RING, not (first and u == 0))
                    if not (first and u < 2):
                        send(base + u - 2, (u - 2) % RING)

            for j in range(AHEAD):
                gather(j, j, False)
            tiles(0, True)
            with pool.Fori(1, MT // RING) as i:
                tiles(i * RING, False)
            for u in range(2):
                send(MT - 2 + u, RING - 2 + u)
            for r in range(RING):
                pool.wait_ge(gathered[r], 16 * (MT // RING + (r < AHEAD)))

        @block.tensor
        def _(pe):
            pe.wait_ge(masks, 4)
            pe.wait_ge(w_in, 16 * N_W)
            for c in range(KC):
                for m in range(KC):
                    last = pe.transpose(bank[:, 6, c * D + m * P:c * D + (m + 1) * P],
                                        wq_nat[:, m, c * P:(c + 1) * P], ident[:, :])
            last.then_inc(w_ps, 1)
            for c in range(KC):
                last = pe.transpose(bank[:, 5, c * 48:(c + 1) * 48], wvrk_nat[0:48, c * P:(c + 1) * P],
                                    ident[0:48, 0:48])
            last.then_inc(w_ps, 1)
            for c in range(KC):
                for m in range(KC):
                    last = pe.transpose(bank[:, 7, c * D + m * P:c * D + (m + 1) * P],
                                        wo_nat[:, m, c * P:(c + 1) * P], ident[:, :])
            last.then_inc(w_ps, 1)

            def transpose_x(g):
                if g:
                    pe.wait_ge(xT_act, g)
                    pe.wait_ge(xT_dve, g)
                for u in range(GT):
                    pe.wait_ge(xn_ready, GT * g + u + 1)
                    for c in range(KC):
                        t = pe.transpose(bank[:, c, u * P:(u + 1) * P], xn[:, g % 2, u, c * P:(c + 1) * P],
                                         ident[:, :])
                        if u == GT - 1:
                            t.then_inc(xT_ps, 1)

            def project(g):
                pe.wait_ge(xT_act, g + 1)
                pe.wait_ge(xT_dve, g + 1)
                if g:
                    pe.wait_ge(vr_ready, g)
                    pe.wait_ge(kl_ready, g)
                for c in range(KC):
                    mm = pe.matmul(bank[0:48, 2, :], wvrkT[:, c, :], xnT[:, g % 2, c, :],
                                   start=(c == 0), stop=(c == KC - 1))
                mm.then_inc(proj_ps, 1)
                for m in range(KC):
                    if g:
                        pe.wait_ge(ql_ready, KC * (g - 1) + m + 1)
                    for c in range(KC):
                        mm = pe.matmul(bank[:, 3 + m, :], wqT[:, c, m * P:(m + 1) * P], xnT[:, g % 2, c, :],
                                       start=(c == 0), stop=(c == KC - 1))
                    mm.then_inc(proj_ps, 1)

            transpose_x(0)
            pe.wait_ge(w_act, 2)
            for g in range(NG):
                project(g)
                if g < NG - 1:
                    transpose_x(g + 1)
                pe.wait_ge(vr_ready, g + 1)
                if g:
                    pe.wait_ge(vl_ready, g)
                for u in range(GT):
                    t = pe.transpose(bank[:, 5, u * 32:(u + 1) * 32], vr[0:32, u * P:(u + 1) * P],
                                     ident[0:32, 0:32])
                t.then_inc(vrT_ps, 1)

            pe.wait_ge(w_act, 2)
            pe.wait_ge(w_dve, 1)
            pe.wait_ge(masks, 11)
            pe.wait_ge(chosen_ready, 1)
            flat = chosen[:].rearrange("p t e -> p (t e)")
            pe.matmul(bank[:, 6, 0:NT * E], below[:, :], flat, start=True, stop=True).then_inc(place_ps, 1)
            pe.matmul(bank[:, 7, 0:NT * E], ones_b[:, :], flat, start=True, stop=True).then_inc(place_ps, 1)

            def scores_for_max(b, buf, n):
                pair, qt = n // 2, n % 2
                if n == 0:
                    pe.wait_ge(q_in[buf][0], 64 * (b // 2 + 1) if isinstance(b, int) else (b - buf) * 32 + 64)
                if n == 8:
                    pe.wait_ge(q_in[buf][1], 64 * (b // 2 + 1) if isinstance(b, int) else (b - buf) * 32 + 64)
                if not (isinstance(b, int) and b == 0 and n < 2):
                    pe.wait_ge(max_done, b * 16 + (n - 1))
                A = bank[:, n % 2, :]
                for k in range(2):
                    pe.matmul(A[:, k * S:(k + 1) * S], qs[:, buf, 2 * pair + k, qt * P:(qt + 1) * P],
                              k_all[:, bass.ds(b * S, S)], start=(k == 0), stop=True, skip_group_check=True)
                diag = A.rearrange("p (k t) -> p k t", k=2)[:, :, qt * P:(qt + 1) * P]
                pe.matmul(diag, ident_b[:, :], mask_q[:], start=False, stop=True,
                          skip_group_check=True).then_inc(p1_ps, 1)

            def transpose_max(b, buf):
                pe.wait_ge(max_done, b * 16 + 16)
                for qt in range(2):
                    t = pe.transpose(bank[0:H, 7, qt * P:(qt + 1) * P], nmax[:, buf, qt, :], ident[:, :])
                t.then_inc(mt_ps, 1)

            def scores(b, buf, q, r):
                n = 3 * q + r
                if not (isinstance(b, int) and b == 0 and n < 2):
                    pe.wait_ge(exp_done, b * 12 + (n - 1))
                A = bank[:, 2 + n % 2, :]
                if r < 2:
                    h0 = 4 * q + 2 * r
                    pe.matmul(A, ks[:, buf, 0:P], qs[:, buf, h0:h0 + 2, :], start=True, stop=True)
                    diag = A.rearrange("p (k t) -> p k t", k=2)[:, :, 0:P]
                    mm = pe.matmul(diag, ident_b[:, :], mask_k[:, 0:2, :], start=False, stop=True,
                                   skip_group_check=True)
                else:
                    pe.matmul(A, ks[:, buf, P:2 * P], qs[:, buf, 4 * q:4 * q + 4, P:2 * P],
                              start=True, stop=True)
                    mm = pe.matmul(A, ident_b[:, :], mask_k[:], start=False, stop=True, skip_group_check=True)
                mm.then_inc(s_ps, 1)

            def weigh_v(b, buf, q):
                pe.wait_ge(exp_done, b * 12 + (3 * q + 3))
                if not (isinstance(b, int) and b == 0 and q < 2):
                    pe.wait_ge(ct_ready, b * NQ + (q - 1))
                o = bank[:, 4 + q % 2, :]
                for j in range(4):
                    pe.matmul(o[32 * j:32 * j + 32, 0:S], vs[:, buf, 0, :],
                              pt[:, (3 * q + j // 2) % 6, (j % 2) * S:(j % 2 + 1) * S], start=True, stop=True)
                for j in range(4):
                    mm = pe.matmul(o[32 * j:32 * j + 32, P:S], vs[:, buf, 1, :],
                                   pt[:, (3 * q + 2) % 6, j * P:(j + 1) * P], start=False, stop=True,
                                   skip_group_check=True)
                mm.then_inc(pv_ps, 1)

            def context(b, buf, qt):
                if qt == 0:
                    pe.wait_ge(ct_ready, b * NQ + NQ)
                if not (isinstance(b, int) and b == 0 and qt == 0):
                    pe.wait_ge(ctx_ready, b * 2 + qt)
                for q in range(NQ):
                    t = pe.transpose(bank[:, 6, q * P:(q + 1) * P], ct[:, buf, q, qt * P:(qt + 1) * P],
                                     ident[:, :])
                t.then_inc(c_ps, 1)

            def transpose_context(b, qt):
                pe.wait_ge(ctx_ready, b * 2 + (qt + 1))
                for c in range(KC):
                    t = pe.transpose(bank[:, 7, c * P:(c + 1) * P], ctx_n[:, c * P:(c + 1) * P], ident[:, :])
                t.then_inc(t_ps, 1)

            def project_out(b, qt):
                pe.wait_ge(cxt_ready, b * 2 + (qt + 1))
                for c in range(KC):
                    mm = pe.matmul(bank[:, 7, 0:D], cxt[:, c, :], woT[:, c, :], start=(c == 0),
                                   stop=(c == KC - 1))
                mm.then_inc(o_ps, 1)

            def batch(b, buf, first=False, ahead=True):
                pe.wait_ge(m_in[buf], 32 * (b // 2 + 1) if isinstance(b, int) else (b - buf) * 16 + 32)
                pe.wait_ge(kv_ready, b * 2 + 2)
                other = 1 - buf
                n = 0
                for q in range(NQ):
                    if not first:
                        if q == 1:
                            context(b - 1, other, 0)
                        if q == 2:
                            project_out(b - 1, 0)
                    scores(b, buf, q, 0)
                    scores(b, buf, q, 1)
                    if ahead:
                        for _ in range([3, 3, 4, 0][q]):
                            scores_for_max(b + 1, other, n)
                            n += 1
                    if not first and q == 2:
                        context(b - 1, other, 1)
                    if q:
                        weigh_v(b, buf, q - 1)
                    elif not first:
                        weigh_v(b - 1, other, NQ - 1)
                    if not first and q == 3:
                        if ahead:
                            pe.wait_ge(mtl_ready, b + 2)
                        else:
                            pe.wait_ge(o_added, b * 2 - 1)
                        transpose_context(b - 1, 1)
                    scores(b, buf, q, 2)
                    if ahead:
                        for _ in range([3, 3, 0, 0][q]):
                            scores_for_max(b + 1, other, n)
                            n += 1
                    if not first and q == 1:
                        pe.wait_ge(mtl_ready, b + 1)
                        if not (isinstance(b, int) and b == 1):
                            pe.wait_ge(o_added, b * 2 - 2)
                        transpose_context(b - 1, 0)
                    if q == 2 and ahead:
                        if first:
                            pe.wait_ge(mtl_ready, 1)
                        else:
                            pe.wait_ge(o_added, b * 2 - 1)
                        transpose_max(b + 1, other)
                    if not first and q == 3:
                        project_out(b - 1, 1)

            pe.wait_ge(masks, 16)
            pe.wait_ge(qs_padded, 1)
            pe.wait_ge(k_all_in, 64)
            pe.wait_ge(route_ready, 1)
            for n in range(16):
                scores_for_max(0, 0, n)
            transpose_max(0, 0)
            batch(0, 0, first=True)
            batch(1, 1)
            with pe.Fori(1, B // 2 - 1) as i:
                batch(i * 2, 0)
                batch(i * 2 + 1, 1)
            batch(B - 2, 0)
            batch(B - 1, 1, ahead=False)
            weigh_v(B - 1, 1, NQ - 1)
            context(B - 1, 1, 0)
            pe.wait_ge(o_added, 2 * B - 2)
            transpose_context(B - 1, 0)
            project_out(B - 1, 0)
            context(B - 1, 1, 1)
            pe.wait_ge(o_added, 2 * B - 1)
            transpose_context(B - 1, 1)
            project_out(B - 1, 1)

            pe.wait_ge(experts_in, 16 * N_EXP)
            pe.wait_ge(tile_e_ready, 1)
            pe.wait_ge(exp_done, 12 * B)
            pe.wait_ge(ct_ready, NQ * B)

            def tile_xT(j, r, came):
                pe.wait_ge(gathered[r], came)
                for c in range(KC):
                    t = pe.transpose(bank[:, 0, c * P:(c + 1) * P], xg[:, r, c * P:(c + 1) * P], ident[:, :])
                t.then_inc(xgT_ps, 1)

            def expert(j):
                return pe.value_load(tile_e[0:1, bass.ds(j, 1)], min_val=0, max_val=E - 1)

            def tile_gate_up(j, buf, e):
                pe.wait_ge(xgT_ready, j + 1)
                for c in range(KC):
                    mm = pe.matmul(bank[:, 1 + buf, :], xT[:, buf, c, :],
                                   wgu[:, bass.ds(e * KC + c, 1), :], start=(c == 0), stop=(c == KC - 1))
                mm.then_inc(gu_ps, 1)

            def tile_hT(j, buf):
                pe.wait_ge(h_ready, j + 1)
                for c in range(FC):
                    t = pe.transpose(bank[:, 3, c * P:(c + 1) * P], hh[:, buf, c * P:(c + 1) * P], ident[:, :])
                t.then_inc(hT_ps, 1)

            def tile_down(j, buf, e):
                pe.wait_ge(hT_ready, j + 1)
                for c in range(FC):
                    mm = pe.matmul(bank[:, 4 + buf, 0:D], hT[:, buf, c, :],
                                   wdn[:, bass.ds(e * FC + c, 1), :], start=(c == 0), stop=(c == FC - 1))
                mm.then_inc(dn_ps, 1)

            def tiles(base, turn, first):
                es = {}
                for u in range(RING):
                    j = base + u
                    es[u] = expert(j)
                    tile_gate_up(j, u % 2, es[u])
                    if not (first and u < 2) and u < 2:
                        es[u - 2] = expert(j - 2)
                    tile_xT(j + 1, (u + 1) % RING, turn * 16 + (32 if u == RING - 1 else 16))
                    if not (first and u < 2):
                        tile_down(j - 2, u % 2, es[u - 2])
                    if not (first and u == 0):
                        tile_hT(j - 1, (u + 1) % 2)

            tile_xT(0, 0, 16)
            tiles(0, 0, True)
            with pe.Fori(1, MT // RING) as i:
                tiles(i * RING, i, False)
            e0, e1 = expert(MT - 2), expert(MT - 1)
            pe.wait_ge(y_ready, MT - 3)
            tile_down(MT - 2, 0, e0)
            tile_hT(MT - 1, 1)
            pe.wait_ge(y_ready, MT - 2)
            tile_down(MT - 1, 1, e1)

        @block.scalar
        def _(act):
            act.wait_ge(w_in, 16 * N_W)
            act.wait_ge(w_ps, 2)
            act.activation(wqT[:].rearrange("p c e -> p (c e)"), bank[:, 6, :], ACT.Copy,
                           scale=QSCALE).then_inc(w_act, 1)
            act.activation(wvrkT[:].rearrange("p c e -> p (c e)"), bank[:, 5, 0:KC * 48],
                           ACT.Copy).then_inc(w_act, 1)
            act.wait_ge(var_ready, 1)
            act.activation(std0[:, :], var_e[:, :], ACT.Sqrt).then_inc(std_ready, 1)

            for g in range(NG):
                act.wait_ge(xT_ps, 2 * g + 1)
                if g >= 2:
                    act.wait_ge(proj_ps, 3 * (g - 1))
                act.activation(xnT[:, g % 2, 0, :], bank[:, 0, :], ACT.Copy).then_inc(xT_act, 1)
                act.wait_ge(proj_ps, 3 * g + 1)
                if g:
                    act.wait_ge(vrT_ps, g)
                act.activation(vr[0:32, :], bank[0:32, 2, :], ACT.Identity, bias=bvrk[0:32, :]
                               ).then_inc(vr_ready, 1)
                if g:
                    act.wait_ge(k_stored, 32 * g)
                act.activation(khl[32:48, 0, :], bank[32:48, 2, :], ACT.Identity, bias=bvrk[32:48, :]
                               ).then_inc(kh_ready, 1)
                if g:
                    act.wait_ge(q_stored, 32 * g)
                else:
                    act.wait_ge(w_ps, 3)
                    act.wait_ge(w_dve, 2)
                for m in range(KC):
                    act.wait_ge(proj_ps, 3 * g + 2 + m)
                    act.activation(qhl[:, 0, m, :], bank[:, 3 + m, :], ACT.Identity, bias=bq_s[:, m:m + 1]
                                   ).then_inc(qh_ready, 1)

            act.wait_ge(shifted, 1)
            act.activation(probs[:], logits[:], ACT.Exp).then_inc(exped, 1)

            def exp_scores(b, n):
                act.wait_ge(s_ps, b * 12 + (n + 1))
                if not (isinstance(b, int) and b == 0 and n < 6):
                    act.wait_ge(pv_ps, b * NQ + (n // 3 - 1))
                act.activation(pt[:, n % 6, :], bank[:, 2 + n % 2, :], ACT.Exp).then_inc(exp_done, 1)

            def keep_context(b, buf, q):
                act.wait_ge(pv_ps, b * NQ + (q + 1))
                if not (isinstance(b, int) and b < 2):
                    act.wait_ge(c_ps, b * 2 - 2)
                act.activation(ct[:, buf, q, :], bank[:, 4 + q % 2, 0:S], ACT.Copy).then_inc(ct_ready, 1)

            def keep_cxt(b, qt):
                act.wait_ge(t_ps, b * 2 + (qt + 1))
                if not (isinstance(b, int) and b == 0 and qt == 0):
                    act.wait_ge(o_ps, b * 2 + qt)
                act.activation(cxt[:].rearrange("p c t -> p (c t)"), bank[:, 7, 0:D], ACT.Copy
                               ).then_inc(cxt_ready, 1)

            def keep_max(b, buf):
                act.wait_ge(mt_ps, b + 1)
                act.activation(mt[:, buf, 0, :], bank[0:H, 7, 0:S], ACT.Copy).then_inc(mth_ready, 1)

            def batch(b, buf, first=False, ahead=True):
                other = 1 - buf
                for q in range(NQ):
                    if q == 2 and not first:
                        keep_cxt(b - 1, 0)
                    exp_scores(b, 3 * q)
                    exp_scores(b, 3 * q + 1)
                    if q:
                        keep_context(b, buf, q - 1)
                    elif not first:
                        keep_context(b - 1, other, NQ - 1)
                    if q == 3 and not first:
                        keep_cxt(b - 1, 1)
                    exp_scores(b, 3 * q + 2)
                    if q == 2 and ahead:
                        keep_max(b + 1, other)

            for c4 in range(4):
                es = slice(c4 * E // 4, (c4 + 1) * E // 4)
                gs = slice(es.start * KC, es.stop * KC)
                act.dma_start(wgu[:, gs, 0:F], wgate[es].rearrange("e (c p) f -> p (e c) f", p=P)
                              ).then_inc(experts_in, 16)
                act.dma_start(wgu[:, gs, F:2 * F], wup[es].rearrange("e (c p) f -> p (e c) f", p=P)
                              ).then_inc(experts_in, 16)
                act.dma_start(wdn[:, gs, :], wdown[es].rearrange("e (c p) f -> p (e c) f", p=P)
                              ).then_inc(experts_in, 16)

            keep_max(0, 0)
            act.wait_ge(tile_e_ready, 1)
            batch(0, 0, first=True)
            batch(1, 1)
            with act.Fori(1, B // 2 - 1) as i:
                batch(i * 2, 0)
                batch(i * 2 + 1, 1)
            batch(B - 2, 0)
            batch(B - 1, 1, ahead=False)
            keep_context(B - 1, 1, NQ - 1)
            keep_cxt(B - 1, 0)
            keep_cxt(B - 1, 1)

            def tile_silu(j, buf):
                act.wait_ge(gu_ps, j + 1)
                act.activation(sg[:, buf, :], bank[:, 1 + buf, 0:F], ACT.Silu).then_inc(silu_ready, 1)

            def tile_xT(j, buf):
                act.wait_ge(xgT_ps, j + 1)
                act.activation(xT[:, buf].rearrange("p c t -> p (c t)"), bank[:, 0, 0:D], ACT.Copy
                               ).then_inc(xgT_ready, 1)

            def tile_y(j, r, sent):
                act.wait_ge(dn_ps, j + 1)
                if sent is not None:
                    act.wait_ge(y_sent[r], sent)
                act.activation(ys[:, r, :], bank[:, 4 + r % 2, 0:D], ACT.Copy).then_inc(y_ready, 1)

            def tiles(base, turn, first):
                for u in range(RING):
                    j = base + u
                    tile_silu(j, u % 2)
                    tile_xT(j + 1, (u + 1) % 2)
                    if u < 2 and not first:
                        tile_y(j - 2, u + 2, None if isinstance(turn, int) and turn == 1 else turn * 16 - 16)
                    elif u >= 2:
                        tile_y(j - 2, u - 2, None if first else turn * 16)

            tile_xT(0, 0)
            tiles(0, 0, True)
            tiles(RING, 1, False)
            with act.Fori(2, MT // RING) as i:
                tiles(i * RING, i, False)
            for u in range(2):
                tile_y(MT - 2 + u, RING - 2 + u, 16 * (MT // RING - 1))

        @block.vector
        def _(dve):
            ln = Steps(dve, dve_ln)
            for t in range(NT):
                dve.wait_ge(x_in[t // GT], 16)
                last = dve.bn_stats(stats[:, t, :], xs[:, t, :])
            ln(last)
            for t in range(NT):
                last = dve.bn_aggr(mv[:, t, :], stats[:, t, :])
            ln(last)
            dve.tensor_scalar(var_e[:, :], mv[:, :, 1], LN_EPS, None, ALU.add).then_inc(var_ready, 1)
            dve.wait_ge(std_ready, 1)
            ln(dve.reciprocal(rstd[:, :], std0[:, :]))
            ln(dve.tensor_tensor(rstd[:, :], rstd[:, :], var_e[:, :], ALU.mult))
            ln(dve.tensor_tensor(rstd[:, :], rstd[:, :], std0[:, :], ALU.add))
            ln(dve.tensor_scalar(rstd[:, :], rstd[:, :], 0.5, None, ALU.mult))
            ln(dve.reciprocal(rstd[:, :], rstd[:, :]))

            def normalise(g):
                if g >= 2:
                    dve.wait_ge(xT_ps, 2 * (g - 1))
                    dve.wait_ge(xn_stored[g % 2], 16 * (g // 2))
                for u in range(GT):
                    t = g * GT + u
                    dve.tensor_scalar(xn[:, g % 2, u, :], xs[:, t, :], mv[:, t, 0:1], rstd[:, t:t + 1],
                                      ALU.subtract, ALU.mult).then_inc(xn_ready, 1)

            normalise(0)
            dve.wait_ge(w_ps, 3)
            dve.tensor_copy(woT[:].rearrange("p c e -> p (c e)"), bank[:, 7, :]).then_inc(w_dve, 1)
            dve.tensor_scalar(bq_s[:, :], bq[:, :], QSCALE, None, ALU.mult).then_inc(w_dve, 1)
            dve.wait_ge(w_dve, 2)
            dve.wait_ge(masks, 15)
            for g in range(NG):
                dve.wait_ge(xT_ps, 2 * g + 2)
                if g >= 2:
                    dve.wait_ge(proj_ps, 3 * (g - 1))
                dve.tensor_copy(xnT[:, g % 2, 1, :], bank[:, 1, :]).then_inc(xT_dve, 1)
                if g < NG - 1:
                    normalise(g + 1)
                dve.wait_ge(kh_ready, g + 1)
                dve.scalar_tensor_tensor(out=khl[32:48, 1, :], in0=bank[32:48, 2, :], scalar=bvrk[32:48, :],
                                         in1=khl[32:48, 0, :].bitcast(F32), op0=ALU.add, op1=ALU.subtract
                                         ).then_inc(kl_ready, 1)
                for m in range(KC):
                    dve.wait_ge(qh_ready, KC * g + m + 1)
                    dve.scalar_tensor_tensor(out=qhl[:, 1, m, :], in0=bank[:, 3 + m, :],
                                             scalar=bq_s[:, m:m + 1], in1=qhl[:, 0, m, :].bitcast(F32),
                                             op0=ALU.add, op1=ALU.subtract).then_inc(ql_ready, 1)
                dve.wait_ge(vrT_ps, g + 1)
                vl = bank[:, 5, 0:GT * 32].rearrange("p (u c) -> p u c", u=GT)
                dve.tensor_copy(v_all[:, g * GT:(g + 1) * GT, 0:HD], vl[:, :, 0:HD])
                dve.tensor_copy(logits[:, g * GT:(g + 1) * GT, :], vl[:, :, HD:HD + E]).then_inc(vl_ready, 1)

            rt = Steps(dve, dve_rt)
            dve.wait_ge(vl_ready, NG)

            def over_e(ap):
                return ap.unsqueeze(2).to_broadcast([P, NT, E])

            rt(dve.tensor_reduce(rowstat[:, :], logits[:], AX.X, ALU.max))
            dve.tensor_tensor(logits[:], logits[:], over_e(rowstat[:, :]), ALU.subtract).then_inc(shifted, 1)
            dve.wait_ge(exped, 1)
            rt(dve.tensor_reduce(rowstat[:, :], probs[:], AX.X, ALU.add))
            rt(dve.reciprocal(rowstat[:, :], rowstat[:, :]))
            rt(dve.tensor_tensor(probs[:], probs[:], over_e(rowstat[:, :]), ALU.mult))
            for t in range(NT):
                last = dve.max(top_w[:, t, :], probs[:, t, :])
            rt(last)
            for t in range(NT):
                last = dve.max_index(top_e[:, t, :], top_w[:, t, :], probs[:, t, :])
            rt(last)
            rt(dve.tensor_reduce(rowstat[:, :], top_w[:, :, 0:TOP_K], AX.X, ALU.add))
            rt(dve.reciprocal(rowstat[:, :], rowstat[:, :]))
            rt(dve.tensor_tensor(coef[:], top_w[:, :, 0:TOP_K],
                                 rowstat[:, :].unsqueeze(2).to_broadcast([P, NT, TOP_K]), ALU.mult))
            rt(dve.tensor_copy(top_ef[:], top_e[:, :, 0:TOP_K]))
            dve.wait_ge(masks, 21)
            choice = onehot.rearrange("p t k e -> p (t k) e")
            rt(dve.tensor_tensor(choice, top_ef[:].rearrange("p t k -> p (t k)").unsqueeze(2).to_broadcast([P, NT * TOP_K, E]),
                                 iota_e[:].unsqueeze(1).to_broadcast([P, NT * TOP_K, E]), ALU.is_equal))
            with nc.allow_low_precision(reason="each sum is 0 or 1"):
                dve.tensor_reduce(chosen[:], onehot.rearrange("p t k e -> p t e k"), AX.X, ALU.add
                                  ).then_inc(chosen_ready, 1)
            dve.wait_ge(place_ps, 2)
            rt(dve.tensor_copy(scan_t[:, 0, PADT:, :], bank[:, 7, 0:NT * E].rearrange("p (t e) -> p t e", t=NT)))
            src, step = 0, 1
            while step < NT:
                rt(dve.tensor_tensor(scan_t[:, 1 - src, PADT:, :], scan_t[:, src, PADT:, :],
                                     scan_t[:, src, PADT - step:PADT + NT - step, :], ALU.add))
                src, step = 1 - src, 2 * step
            count = scan_t[:, src, PADT + NT - 1, :]
            before = scan_t[:, src, PADT - 1:PADT + NT - 1, :]
            rt(dve.tensor_scalar(ntile_i[:, :], count, float(P - 1), None, ALU.add))
            rt(dve.tensor_scalar(ntile_i[:, :], ntile_i[:, :], P.bit_length() - 1, None,
                                 ALU.logical_shift_right))
            rt(dve.tensor_copy(scan_e[:, 0, PADE:], ntile_i[:, :]))
            esrc, step = 0, 1
            while step < E:
                rt(dve.tensor_tensor(scan_e[:, 1 - esrc, PADE:], scan_e[:, esrc, PADE:],
                                     scan_e[:, esrc, PADE - step:PADE + E - step], ALU.add))
                esrc, step = 1 - esrc, 2 * step
            end = scan_e[:, esrc, PADE:]
            rt(dve.tensor_tensor(first_row[:, :], end, ntile_i[:, :], ALU.subtract))
            rt(dve.tensor_scalar(first_row[:, :], first_row[:, :], float(P), None, ALU.mult))
            rt(dve.tensor_tensor(probs[:], before, bank[:, 6, 0:NT * E].rearrange("p (t e) -> p t e", t=NT),
                                 ALU.add))
            rt(dve.tensor_tensor(probs[:], probs[:], first_row[:].unsqueeze(1).to_broadcast([P, NT, E]),
                                 ALU.add))
            for k in range(TOP_K):
                last = dve.tensor_tensor(onehot[:, :, k, :], onehot[:, :, k, :], probs[:], ALU.mult)
            rt(last)
            rt(dve.tensor_reduce(slot_f[:].rearrange("p t k -> p (t k)"), choice, AX.X, ALU.add))
            rt(dve.tensor_copy(slot_i[:], slot_f[:]))
            rt(dve.tensor_scalar(slot_p[:], slot_i[:], P - 1, None, ALU.bitwise_and))
            rt(dve.tensor_scalar(slot_i[:], slot_i[:], P.bit_length() - 1, None, ALU.logical_shift_right))
            rt(dve.tensor_copy(slot_pf[:], slot_p[:]))
            rt(dve.tensor_copy(slot_f[:], slot_i[:]))
            rt(dve.scalar_tensor_tensor(out=slot_f[:], in0=slot_pf[:], scalar=float(MT), in1=slot_f[:],
                                        op0=ALU.mult, op1=ALU.add))
            dve.tensor_copy(slot_i[:], slot_f[:]).then_inc(route_ready, 1)
            rt(dve.tensor_tensor(tile_ge, tile_no[:].unsqueeze(2).to_broadcast([1, MT, E]),
                                 end[0:1].unsqueeze(1).to_broadcast([1, MT, E]), ALU.is_ge))
            rt(dve.tensor_reduce(tile_ef[:], tile_ge, AX.X, ALU.add))
            dve.tensor_scalar(tile_e[:], tile_ef[:], float(E - 1), None, ALU.min).then_inc(tile_e_ready, 1)

            def row_max(b, buf, n):
                pair, qt = n // 2, n % 2
                dve.wait_ge(p1_ps, b * 16 + (n + 1))
                A = bank[:, n % 2, :].rearrange("p (k t) -> p k t", k=2)
                dve.tensor_reduce(nmax[:, buf, qt, 2 * pair:2 * pair + 2], A[:, :, 0:(qt + 1) * P], AX.X, ALU.max,
                                  negate=True).then_inc(max_done, 1)

            def split_max(b, buf):
                dve.wait_ge(mth_ready, b + 1)
                dve.tensor_tensor(mt[:, buf, 1, :], bank[0:H, 7, 0:S], mt[:, buf, 0, :].bitcast(F32),
                                  ALU.subtract).then_inc(mtl_ready, 1)

            def normalise_context(b, qt):
                dve.wait_ge(c_ps, b * 2 + (qt + 1))
                c = bank[:, 6, :].rearrange("p (h v) -> p h v", h=H)
                dve.reciprocal(rden[:, qt, :], c[:, :, HD]).then_inc(rden_ready, 1)
                dve.wait_ge(rden_ready, b * 2 + (qt + 1))
                if not (isinstance(b, int) and b == 0 and qt == 0):
                    dve.wait_ge(t_ps, b * 2 + qt)
                dve.tensor_tensor(ctx_n[:].rearrange("p (h v) -> p h v", h=H), c[:, :, 0:HD],
                                  rden[:, qt, :].unsqueeze(2).to_broadcast([P, H, HD]), ALU.mult
                                  ).then_inc(ctx_ready, 1)

            def add_out(b, qt):
                dve.wait_ge(o_ps, b * 2 + (qt + 1))
                tile = xs[:, bass.ds(b * 2 + qt, 1), :].rearrange("p a d -> p (a d)")
                dve.tensor_tensor(tile, tile, bank[:, 7, 0:D], ALU.add).then_inc(o_added, 1)

            def batch(b, buf, first=False, ahead=True):
                other = 1 - buf

                def maxima(a, z):
                    if ahead:
                        for n in range(a, z):
                            row_max(b + 1, other, n)

                maxima(0, 6)
                if not first:
                    normalise_context(b - 1, 0)
                maxima(6, 12)
                if not first:
                    add_out(b - 1, 0)
                maxima(12, 16)
                if not first:
                    normalise_context(b - 1, 1)
                if ahead:
                    split_max(b + 1, other)
                if not first:
                    add_out(b - 1, 1)

            for n in range(16):
                row_max(0, 0, n)
            split_max(0, 0)
            dve.wait_ge(xb_ready, NT)
            batch(0, 0, first=True)
            batch(1, 1)
            with dve.Fori(1, B // 2 - 1) as i:
                batch(i * 2, 0)
                batch(i * 2 + 1, 1)
            batch(B - 2, 0)
            batch(B - 1, 1, ahead=False)
            for qt in range(2):
                normalise_context(B - 1, qt)
                add_out(B - 1, qt)

            dve.wait_ge(list_in, 16)
            dve.tensor_scalar(get_row[:, :], put_row[:, :], T - 1, None, ALU.bitwise_and).then_inc(rows_ready, 1)

            def tile_h(j, buf):
                dve.wait_ge(silu_ready, j + 1)
                dve.tensor_tensor(hh[:, buf, :], sg[:, buf, :], bank[:, 1 + buf, F:2 * F], ALU.mult
                                  ).then_inc(h_ready, 1)

            def tile_hT(j, buf):
                dve.wait_ge(hT_ps, j + 1)
                dve.tensor_copy(hT[:, buf].rearrange("p c t -> p (c t)"), bank[:, 3, 0:F]).then_inc(hT_ready, 1)

            def tiles(base, first):
                for u in range(RING):
                    tile_h(base + u, u % 2)
                    if not (first and u == 0):
                        tile_hT(base + u - 1, (u + 1) % 2)

            tiles(0, True)
            with dve.Fori(1, MT // RING) as i:
                tiles(i * RING, False)
            tile_hT(MT - 1, 1)

            def combine(t, buf, came, gone):
                dve.wait_ge(y_in[buf], came)
                if gone is not None:
                    dve.wait_ge(out_sent[buf], gone)
                for k in range(TOP_K):
                    prev = xs[:, bass.ds(t, 1), :].rearrange("p a d -> p (a d)") if k == 0 else oc[:, buf]
                    if k:
                        dve.wait_ge(combined, t * (TOP_K - 1) + k)
                    step = dve.scalar_tensor_tensor(
                        out=oc[:, buf], in0=yc[:, buf, k, :],
                        scalar=coef[:, bass.ds(t, 1), k:k + 1].rearrange("p a b -> p (a b)"),
                        in1=prev, op0=ALU.mult, op1=ALU.add)
                    step.then_inc(added if k == TOP_K - 1 else combined, 1)

            for u in range(2):
                combine(u, u, 16, None)
            with dve.Fori(1, NT // 2) as i:
                for u in range(2):
                    combine(i * 2 + u, u, i * 16 + 16, i * 16)


_INS = ['L0_attn_x', 'L0_attn_Wqkv_w', 'L0_attn_Wqkv_b', 'L0_attn_out_w', 'L0_attn_out_b',
        'L0_ffn_w_router', 'L0_ffn_w_gate', 'L0_ffn_w_up', 'L0_ffn_w_down']
_OUTS = [((8, 256, 256), 'float32')]


def kernel(**inputs):
    import numpy as _np
    import concourse.bacc as _bacc
    from concourse import mybir as _mybir
    from concourse.bass_utils import run_bass_kernel_spmd as _run

    nc = _bacc.Bacc("TRN2", target_bir_lowering=False, num_devices=1)
    arrays, args = {}, []
    for name in _INS:
        a = _np.ascontiguousarray(inputs[name])
        arrays[f"in_{name}_dram"] = a
        args.append(nc.dram_tensor(f"in_{name}_dram", a.shape, _mybir.dt.from_np(a.dtype), kind="ExternalInput").ap())
    for i, (shape, dtype) in enumerate(_OUTS):
        dt = _mybir.dt.from_np(_np.dtype(dtype))
        args.append(nc.dram_tensor(f"out_{i}_dram", shape, dt, kind="ExternalOutput").ap())
    attention_and_experts(nc, *args)
    r = _run(nc, [arrays], core_ids=[0])
    return r.results[0]["out_0_dram"]
```

```python
from contextlib import ExitStack

import concourse.bass as bass
from concourse import mybir

ALU = mybir.AluOpType
ACT = mybir.ActivationFunctionType
AX = mybir.AxisListType
F32 = mybir.dt.float32
F32R = mybir.dt.float32r
BF16 = mybir.dt.bfloat16
I32 = mybir.dt.int32
U32 = mybir.dt.uint32

P = 128
TOP_K = 4
LN_EPS = 1e-5
MASKED = -1e30


class Steps:

    def __init__(self, eng, sem):
        self.eng, self.sem, self.n = eng, sem, 0

    def __call__(self, ins):
        self.n += 1
        ins.then_inc(self.sem, 1)
        self.eng.wait_ge(self.sem, self.n)


def attention_and_experts(nc, x, wqkv, bqkv, wout, bout, wrouter, wgate, wup, wdown, out):
    B, S, D = x.shape
    E, _, F = wgate.shape
    T = B * S
    NT = T // P
    HD = (wqkv.shape[0] - D) // 2
    H = D // HD
    KC = D // P
    FC = F // P
    GT = 4
    NG = NT // GT
    GW = GT * P
    NQ = H // 4
    RING = 4
    MT = -(-((T * TOP_K + E * (P - 1)) // P) // RING) * RING
    NOROW = T * TOP_K
    assert (D, S, F, HD, E, KC, FC) == (2 * P, 2 * P, 2 * P, 16, 16, 2, 2) and T & (T - 1) == 0
    VW = 32
    QSCALE = float(HD) ** -0.5

    x_rows = x.rearrange("b s d -> (b s) d")
    out_rows = out.rearrange("b s d -> (b s) d")

    xn_d = nc.dram_tensor("xn_d", (T, D), F32).ap()
    q_d = nc.dram_tensor("q_d", (2, D, T), F32).ap()
    k_d = nc.dram_tensor("k_d", (2, HD, T), F32).ap()
    slots_d = nc.dram_tensor("slots_d", (P * MT, 2), I32).ap()
    y_d = nc.dram_tensor("y_d", (TOP_K * T, D), F32).ap()

    with ExitStack() as ctx:
        def sb(name, shape, dt=F32):
            return ctx.enter_context(nc.sbuf_tensor(name, shape, dt))

        def sem(name):
            return ctx.enter_context(nc.semaphore(name))

        bank = ctx.enter_context(nc.psum_tensor("bank", [P, 8, 512], F32))

        wgu = sb("wgu", [P, E * KC, 2 * F])
        wdn = sb("wdn", [P, E * FC, D])
        xs = sb("xs", [P, NT, D])
        k_all = sb("k_all", [P, T], F32R)
        ks = sb("ks", [P, 2, S], F32R)
        v_all = sb("v_all", [P, NT, VW])
        vs = sb("vs", [P, 2, 2, VW])
        pt = sb("pt", [P, 6, 512])
        ct = sb("ct", [P, 2, NQ, S])
        out_buf = sb("out_buf", [P, 4 * D])
        ctx_n = out_buf[:, 0:2 * D].rearrange("p (a d) -> p a d", a=2)
        cxt = out_buf[:, 2 * D:].rearrange("p (a c t) -> p a c t", a=2, c=KC)
        rden = sb("rden", [P, 2, H])
        nmax = sb("nmax", [P, 2, 2, H])
        mt = sb("mt", [H, 2, 2, S], F32R)
        ident = sb("ident", [P, P])
        ident_b = sb("ident_b", [P, P], BF16)
        below = sb("below", [P, P], BF16)
        ones_b = sb("ones_b", [P, P], BF16)
        mask_q = sb("mask_q", [P, 2, P], BF16)
        mask_k = sb("mask_k", [P, 4, P], BF16)
        wqT = sb("wqT", [P, KC, D])
        wvrkT = sb("wvrkT", [P, KC, 48])
        woT = sb("woT", [P, KC, D])
        bq = sb("bq", [P, KC])
        bq_s = sb("bq_s", [P, KC])
        bvrk = sb("bvrk", [48, 1])
        bo = sb("bo", [P, D])
        stats = sb("stats", [P, NT, 6])
        mv = sb("mv", [P, NT, 2])
        var_e = sb("var_e", [P, NT])
        std0 = sb("std0", [P, NT])
        rstd = sb("rstd", [P, NT])
        logits = sb("logits", [P, NT, E])
        probs = sb("probs", [P, NT, E])
        rowstat = sb("rowstat", [P, NT])
        top_w = sb("top_w", [P, NT, 8])
        top_e = sb("top_e", [P, NT, 8], U32)
        top_ef = sb("top_ef", [P, NT, TOP_K])
        iota_e = sb("iota_e", [P, E])
        onehot = out_buf[:].rearrange("p (t k e) -> p t k e", t=NT, k=TOP_K)
        chosen = sb("chosen", [P, NT, E], BF16)
        PADT = NT // 2
        scan_t = sb("scan_t", [P, 2, PADT + NT, E])
        PADE = E // 2
        scan_e = sb("scan_e", [P, 2, PADE + E])
        ntile_i = sb("ntile_i", [P, E], I32)
        first_row = sb("first_row", [P, E])
        slot_i = sb("slot_i", [P, NT, TOP_K], I32)
        slot_p = sb("slot_p", [P, NT, TOP_K], I32)
        slot_f = sb("slot_f", [P, NT, TOP_K])
        slot_pf = sb("slot_pf", [P, NT, TOP_K])
        row_coef = sb("row_coef", [P, NT, TOP_K, 2], I32)
        tile_no = sb("tile_no", [1, MT])
        tile_ge = scan_t[0:1].rearrange("p a t e -> p (a t e)").bitcast(BF16)[:, 0:MT * E].rearrange("p (j e) -> p j e", j=MT)
        tile_ef = sb("tile_ef", [1, MT])
        tile_e = sb("tile_e", [1, MT], I32)
        scat_to = sb("scat_to", [P, 2, TOP_K], I32)
        scat_val = sb("scat_val", [P, 2, TOP_K, 2], I32)
        slots = sb("slots", [P, MT + RING, 2], I32)
        get_row = sb("get_row", [P, MT + RING], I32)
        get_now = sb("get_now", [P, RING], I32)
        put_now = sb("put_now", [P, RING], I32)

        WORK = 32 * 256
        with nc.sbuf_tensor("early", [P, WORK], F32) as early:
            pass
        with nc.sbuf_tensor("qs", [P, 2, H, S], F32R) as qs:
            pass
        late = sb("late", [P, WORK])

        def carve(region, spans, at=0):
            found = []
            for n in spans:
                found.append(region[:, at:at + n])
                at += n
            assert at <= WORK
            return found

        v_xn, v_xnT, v_qhl, v_khl, v_vr, v_wo = carve(
            early, [2 * GT * D, 2 * KC * GW, 2 * KC * GW, 2 * GW, GW, KC * D])
        xn = v_xn.rearrange("p (b u d) -> p b u d", b=2, u=GT)
        xnT = v_xnT.rearrange("p (b c t) -> p b c t", b=2, c=KC)
        qhl = v_qhl.bitcast(F32R).rearrange("p (a m t) -> p a m t", a=2, m=KC)
        khl = v_khl.bitcast(F32R).rearrange("p (a t) -> p a t", a=2)
        vr = v_vr
        v_wn, = carve(early, [KC * D + D], at=2 * GT * D + 2 * KC * GW)
        wq_nat = v_wn[:, 0:KC * D].rearrange("p (m d) -> p m d", m=KC)
        wvrk_nat = v_wn[:, KC * D:KC * D + D]
        wo_nat = v_wo.rearrange("p (m d) -> p m d", m=KC)
        v_xg, v_xT, v_s, v_h, v_hT, v_y = carve(late, [RING * D, 2 * D, 2 * F, 2 * F, 2 * F, RING * D])
        assert (2 * RING * D + 2 * D + 6 * F) * 2 <= WORK
        xg = v_xg.rearrange("p (r d) -> p r d", r=RING)
        xT = v_xT.rearrange("p (b c t) -> p b c t", b=2, c=KC)
        sg = v_s.rearrange("p (b f) -> p b f", b=2)
        hh = v_h.rearrange("p (b f) -> p b f", b=2)
        hT = v_hT.rearrange("p (b c t) -> p b c t", b=2, c=FC)
        ys = v_y.rearrange("p (r d) -> p r d", r=RING)
        yc = wgu[:].rearrange("p a b -> p (a b)").rearrange("p (t k d) -> p t k d", t=NT, k=TOP_K)

        x_in = [sem(f"x_in{g}") for g in range(NG)]
        w_in = sem("w_in")
        b_in = sem("b_in")
        wo_in = sem("wo_in")
        bo_in = sem("bo_in")
        experts_in = sem("experts_in")
        masks = sem("masks")
        consts = sem("consts")
        w_ps = sem("w_ps")
        w_act = sem("w_act")
        w_dve = sem("w_dve")
        var_ready = sem("var_ready")
        std_ready = sem("std_ready")
        dve_ln = sem("dve_ln")
        xn_ready = sem("xn_ready")
        xb_ready = sem("xb_ready")
        xn_stored = [sem(f"xn_stored{b}") for b in range(2)]
        xT_ps = sem("xT_ps")
        xT_act = sem("xT_act")
        xT_dve = sem("xT_dve")
        proj_ps = sem("proj_ps")
        vr_ready = sem("vr_ready")
        kh_ready = sem("kh_ready")
        kl_ready = sem("kl_ready")
        qh_ready = sem("qh_ready")
        ql_ready = sem("ql_ready")
        q_stored = sem("q_stored")
        k_stored = sem("k_stored")
        vrT_ps = sem("vrT_ps")
        vl_ready = sem("vl_ready")
        k_all_in = sem("k_all_in")
        dve_rt = sem("dve_rt")
        shifted = sem("shifted")
        exped = sem("exped")
        chosen_ready = sem("chosen_ready")
        place_ps = sem("place_ps")
        route_ready = sem("route_ready")
        tile_e_ready = sem("tile_e_ready")
        list_init = sem("list_init")
        init_stored = sem("init_stored")
        scat_copied = sem("scat_copied")
        scattered = [sem(f"scattered{b}") for b in range(2)]
        list_in = sem("list_in")
        rows_ready = sem("rows_ready")
        q_in = [[sem(f"q_in{b}{h}") for h in range(2)] for b in range(2)]
        kv_ready = sem("kv_ready")
        qs_padded = sem("qs_padded")
        p1_ps = sem("p1_ps")
        max_done = sem("max_done")
        mt_ps = sem("mt_ps")
        mth_ready = sem("mth_ready")
        mtl_ready = sem("mtl_ready")
        m_in = [sem(f"m_in{b}") for b in range(2)]
        s_ps = sem("s_ps")
        exp_done = sem("exp_done")
        pv_ps = sem("pv_ps")
        ct_ready = sem("ct_ready")
        c_ps = sem("c_ps")
        rden_ready = sem("rden_ready")
        ctx_ready = sem("ctx_ready")
        t_ps = sem("t_ps")
        cxt_ready = sem("cxt_ready")
        o_ps = sem("o_ps")
        o_added = sem("o_added")
        now_ready = sem("now_ready")
        pool_gate = sem("pool_gate")
        put_ready = sem("put_ready")
        gathered = [sem(f"gathered{r}") for r in range(RING)]
        y_sent = [sem(f"y_sent{r}") for r in range(RING)]
        xgT_ps = sem("xgT_ps")
        xgT_ready = sem("xgT_ready")
        gu_ps = sem("gu_ps")
        silu_ready = sem("silu_ready")
        h_ready = sem("h_ready")
        hT_ps = sem("hT_ps")
        hT_ready = sem("hT_ready")
        dn_ps = sem("dn_ps")
        y_ready = sem("y_ready")
        y_in = [sem(f"y_in{t}") for t in range(NT)]
        combined = sem("combined")
        added = sem("added")
        out_sent = sem("out_sent")

        XT_BANK = [0, 6]
        LN_PARTS = [slice(0, GT), slice(GT, NT)]
        N_W = 4
        N_EXP = 12

        block = ctx.enter_context(nc.Block())

        def max_banks(b):
            return 6 if isinstance(b, int) and b == 0 else 2

        def load_y(queue, t):
            queue.dma_start(yc[:, t], y_d.rearrange("(k t) d -> t k d", k=TOP_K)[t * P:(t + 1) * P]
                            ).then_inc(y_in[t], 16)

        @block.sync
        def _(sp):
            def load_x(g):
                sp.dma_start(xs[:, g * GT:(g + 1) * GT, :],
                             x_rows[g * GW:(g + 1) * GW, :].rearrange("(u p) d -> p u d", p=P)
                             ).then_inc(x_in[g], 16)

            def column(bias):
                return bias.rearrange("(p a) -> p a", a=1)

            load_x(0)
            sp.dma_start(wq_nat, wqkv[0:D, :].rearrange("(m p) d -> p m d", p=P)).then_inc(w_in, 16)
            sp.dma_start(wvrk_nat[0:16, :], wqkv[D + HD:D + 2 * HD, :]).then_inc(w_in, 16)
            sp.dma_start(wvrk_nat[16:32, :], wrouter).then_inc(w_in, 16)
            sp.dma_start(wvrk_nat[32:48, :], wqkv[D:D + HD, :]).then_inc(w_in, 16)
            load_x(1)
            for m in range(KC):
                sp.dma_start(bq[:, m:m + 1], column(bqkv[m * P:(m + 1) * P])).then_inc(b_in, 16)
            sp.wait_ge(consts, 1)
            sp.dma_start(bvrk[0:16, :], column(bqkv[D + HD:D + 2 * HD])).then_inc(b_in, 16)
            sp.dma_start(bvrk[32:48, :], column(bqkv[D:D + HD])).then_inc(b_in, 16)
            sp.dma_start(wo_nat, wout.rearrange("(m p) d -> p m d", p=P)).then_inc(wo_in, 16)
            load_x(2)
            load_x(3)
            sp.dma_start(bo[:, :], bout.partition_broadcast(P)).then_inc(bo_in, 16)

            def load_k(start, stop):
                sp.wait_ge(k_stored, 32 * (stop // GW))
                for r in range(4):
                    sp.dma_start(k_all[16 * r:16 * r + 16, start:stop].bitcast(F32), k_d[r // 2, :, start:stop]
                                 ).then_inc(k_all_in, 16)

            for g in range(NG):
                cols = slice(g * GW, (g + 1) * GW)
                sp.wait_ge(xn_ready, GT * (g + 1))
                sp.dma_start(xn_d[cols, :].rearrange("(u p) d -> p u d", p=P), xn[:, g % 2]
                             ).then_inc(xn_stored[g % 2], 16)
                sp.wait_ge(kl_ready, g + 1)
                for a in range(2):
                    sp.dma_start(k_d[a, :, cols], khl[32:48, a, :].bitcast(F32)).then_inc(k_stored, 16)
                sp.wait_ge(ql_ready, KC * (g + 1))
                for a in range(2):
                    sp.dma_start(q_d[a, :, cols].rearrange("(m p) t -> p m t", p=P), qhl[:, a].bitcast(F32)
                                 ).then_inc(q_stored, 16)
                if g == 1:
                    load_k(0, GW)
            sp.wait_ge(list_init, 1)
            sp.dma_start(slots_d.rearrange("(p j) a -> p (j a)", p=P), slots[:, 0:MT, :].rearrange("p j a -> p (j a)")).then_inc(init_stored, 16)

            def load_q(b, buf, half):
                hs = slice(half * H // 2, (half + 1) * H // 2)
                for r in range(4):
                    src = q_d[r % 2].rearrange("(h d) t -> d h t", d=HD)[:, hs, bass.ds(b * S, S)]
                    sp.dma_start(qs[16 * r:16 * r + 16, buf, hs, :].bitcast(F32), src).then_inc(q_in[buf][half], 16)

            def load_m(b, buf):
                sp.wait_ge(mtl_ready, b + 1)
                for a in range(2):
                    sp.dma_start(qs[64 + a:65 + a, buf, :, :].bitcast(F32), mt[:, buf, a, :].bitcast(F32)).then_inc(m_in[buf], 16)

            def during(b, buf):
                sp.wait_ge(s_ps, b * 12 + 6)
                load_q(b + 2, buf, 0)
                load_m(b + 1, 1 - buf)
                sp.wait_ge(s_ps, b * 12 + 12)
                load_q(b + 2, buf, 1)

            for r in range(2):
                sp.wait_ge(xn_stored[r], 16 * NG // 2)
            sp.wait_ge(vrT_ps, NG)
            sp.wait_ge(q_stored, 32)
            for half in range(2):
                load_q(0, 0, half)
            load_k(GW, T)
            sp.wait_ge(q_stored, 32 * NG)
            sp.wait_ge(w_ps, 3)
            for half in range(2):
                load_q(1, 1, half)
            sp.wait_ge(qs_padded, 2)
            load_m(0, 0)
            with sp.Fori(0, B // 2 - 2) as i:
                for u in range(2):
                    during(i * 2 + u, u)
            for u in range(2):
                during(B - 4 + u, u)
            load_m(B - 1, 1)
            for b in range(2):
                sp.wait_ge(scattered[b], 16 * TOP_K * NT // 2)
            sp.dma_start(slots[:, 0:MT, :].rearrange("p j a -> p (j a)"),
                         slots_d.rearrange("(p j) a -> p (j a)", p=P)).then_inc(list_in, 16)

            for r in range(RING):
                sp.wait_ge(y_sent[r], 16 * (MT // RING))
            for t in range(0, NT, 2):
                load_y(sp, t)
            for t in range(NT):
                sp.wait_ge(added, t + 1)
                sp.dma_start(out_rows[t * P:(t + 1) * P, :], xs[:, t, :]).then_inc(out_sent, 16)
            sp.wait_ge(out_sent, 16 * NT)

        @block.gpsimd
        def _(pool):
            const = Steps(pool, masks)
            pool.memset(bvrk[:, :], 0.0).then_inc(consts, 1)
            pool.wait_ge(consts, 1)
            for t in (ident, ident_b):
                const(pool.memset(t[:, :], 0.0))
            for t in (ident, ident_b):
                const(pool.affine_select(out=t[:, :], in_=t[:, :], compare_op=ALU.not_equal, fill=1.0, base=0,
                                   pattern=[[-1, P]], channel_multiplier=1))
            const(pool.memset(mask_q[:], 0.0))
            const(pool.memset(mask_k[:], 0.0))
            const(pool.memset(below[:], 1.0))
            const(pool.affine_select(out=mask_q[:], in_=mask_q[:], compare_op=ALU.is_ge, fill=MASKED, base=0,
                               pattern=[[0, 2], [-1, P]], channel_multiplier=1))
            const(pool.affine_select(out=mask_k[:], in_=mask_k[:], compare_op=ALU.is_ge, fill=MASKED, base=0,
                               pattern=[[0, 4], [1, P]], channel_multiplier=-1))
            const(pool.affine_select(out=below[:], in_=below[:], compare_op=ALU.is_ge, fill=0.0, base=-1,
                               pattern=[[1, P]], channel_multiplier=-1))
            const(pool.memset(ones_b[:], 1.0))
            const(pool.memset(k_all[64:128].bitcast(F32), 0.0))
            const(pool.memset(ks[64:128].bitcast(F32), 0.0))
            const(pool.memset(v_all[:, :, HD + 1:VW], 0.0))
            const(pool.memset(v_all[:, :, HD:HD + 1], 1.0))
            const(pool.memset(ks[64:66].bitcast(F32), 1.0))
            const(pool.memset(scan_t[:], 0.0))
            const(pool.memset(scan_e[:], 0.0))
            const(pool.iota(iota_e[:], [[1, E]], base=0, channel_multiplier=0,
                      allow_small_or_imprecise_dtypes=True))
            const(pool.iota(row_coef[:, :, :, 0], [[P, NT], [T, TOP_K]], base=0, channel_multiplier=1))
            const(pool.iota(tile_no[:], [[1, MT]], base=0, channel_multiplier=0,
                      allow_small_or_imprecise_dtypes=True))
            pool.iota(slots[:], [[0, MT + RING], [-NOROW, 2]], base=NOROW, channel_multiplier=0
                      ).then_inc(list_init, 1)

            pool.wait_ge(bo_in, 16)
            for t in range(NT):
                pool.wait_ge(xn_ready, t + 1)
                pool.tensor_tensor(xs[:, t, :], xs[:, t, :], bo[:, :], ALU.add).then_inc(xb_ready, 1)

            def copy_kv(b, buf):
                if isinstance(b, int) and b < 2:
                    pool.wait_ge(k_all_in, 64)
                else:
                    pool.wait_ge(kv_ready, b * 2)
                pool.tensor_copy(ks[0:64, buf, :], k_all[0:64, bass.ds(b * S, S)]).then_inc(kv_ready, 1)
                pool.wait_ge(kv_ready, b * 2 + 1)
                pool.tensor_copy(vs[:, buf], v_all[:, bass.ds(b * 2, 2), :]).then_inc(kv_ready, 1)

            pool.wait_ge(vrT_ps, NG)
            for r in range(2):
                pool.wait_ge(xn_stored[r], 16 * NG // 2)
            pool.wait_ge(xb_ready, NT)
            pool.memset(qs[64:128, 0].bitcast(F32), 0.0).then_inc(qs_padded, 1)
            pool.wait_ge(qs_padded, 1)
            pool.wait_ge(vl_ready, NG)
            copy_kv(0, 0)
            pool.wait_ge(kv_ready, 2)
            pool.wait_ge(w_ps, 3)
            pool.wait_ge(q_stored, 32 * NG)
            pool.wait_ge(k_stored, 32 * NG)
            pool.memset(qs[64:128, 1].bitcast(F32), 0.0).then_inc(qs_padded, 1)
            pool.wait_ge(qs_padded, 2)
            copy_kv(1, 1)

            pool.wait_ge(kv_ready, 4)
            pool.wait_ge(init_stored, 16)
            pool.wait_ge(route_ready, 1)
            last_slot = pool.to_reg(P * MT - 1)

            def copied(sem, value):
                pool.wait_ge(sem, value)
                pool.sem_inc(pool_gate, 1)

            def scatter_slots(t, buf, used):
                if used is not None:
                    pool.wait_ge(scattered[buf], used)
                pool.tensor_copy(scat_to[:, buf, :], slot_i[:, bass.ds(t, 1), :]).then_inc(scat_copied, 1)
                pool.tensor_copy(scat_val[:, buf], row_coef[:, bass.ds(t, 1)].rearrange("p a k b -> p (a k) b")).then_inc(scat_copied, 1)
                for k in range(TOP_K):
                    if k == 0:
                        copied(scat_copied, t * 2 + 2)
                    pool.indirect_dma_start(
                        slots_d, bass.IndirectOffsetOnAxis(ap=scat_to[:, buf, k:k + 1], axis=0),
                        scat_val[:, buf, k, :], None, bounds_check=last_slot, oob_is_err=False,
                    ).then_inc(scattered[buf], 16)

            def next_kv(b, buf):
                pool.wait_ge(pv_ps, (b - 1) * NQ)
                copy_kv(b, buf)

            pool.wait_ge(k_all_in, 128)
            for t in range(4):
                scatter_slots(t, t % 2, 16 * TOP_K * (t // 2) if t >= 2 else None)
            with pool.Fori(1, B // 2) as i:
                for u in range(2):
                    next_kv(i * 2 + u, u)
                    for v in range(2):
                        scatter_slots(i * 4 + (2 * u + v), v, (i * 2 + u) * (16 * TOP_K))
            assert NT == 4 + 4 * (B // 2 - 1)

            pool.wait_ge(kv_ready, 2 * B)
            pool.wait_ge(rows_ready, 1)
            last_row = pool.to_reg(T - 1)
            last_out = pool.to_reg(T * TOP_K - 1)
            pool.wait_ge(s_ps, 12 * (B - 1))

            def gather(j, r, wait):
                if wait:
                    pool.wait_ge(xgT_ps, j - RING + 1)
                pool.tensor_copy(get_now[:, r:r + 1], get_row[:, bass.ds(j, 1)]).then_inc(now_ready, 1)
                copied(now_ready, j + 1)
                pool.indirect_dma_start(
                    xg[:, r, :], None, xn_d, bass.IndirectOffsetOnAxis(ap=get_now[:, r:r + 1], axis=0),
                    bounds_check=last_row, oob_is_err=False).then_inc(gathered[r], 16)

            def send(j, r):
                pool.wait_ge(y_ready, j + 1)
                pool.tensor_copy(put_now[:, r:r + 1], slots[:, bass.ds(j, 1), 0]).then_inc(put_ready, 1)
                copied(put_ready, j + 1)
                pool.indirect_dma_start(
                    y_d, bass.IndirectOffsetOnAxis(ap=put_now[:, r:r + 1], axis=0), ys[:, r, :], None,
                    bounds_check=last_out, oob_is_err=False).then_inc(y_sent[r], 16)

            AHEAD = RING - 1

            def tiles(base, first):
                for u in range(RING):
                    gather(base + u + AHEAD, (u + AHEAD) % RING, not (first and u == 0))
                    if not (first and u < 2):
                        send(base + u - 2, (u - 2) % RING)

            for j in range(AHEAD):
                gather(j, j, False)
            tiles(0, True)
            with pool.Fori(1, MT // RING) as i:
                tiles(i * RING, False)
            for u in range(2):
                send(MT - 2 + u, RING - 2 + u)
            for r in range(RING):
                pool.wait_ge(gathered[r], 16 * (MT // RING + (r < AHEAD)))

        @block.tensor
        def _(pe):
            pe.wait_ge(masks, 4)
            pe.wait_ge(w_in, 16 * N_W)
            for c in range(KC):
                for m in range(KC):
                    last = pe.transpose(bank[:, 6, c * D + m * P:c * D + (m + 1) * P],
                                        wq_nat[:, m, c * P:(c + 1) * P], ident[:, :])
            last.then_inc(w_ps, 1)
            for c in range(KC):
                last = pe.transpose(bank[:, 5, c * 48:(c + 1) * 48], wvrk_nat[0:48, c * P:(c + 1) * P],
                                    ident[0:48, 0:48])
            last.then_inc(w_ps, 1)
            def transpose_x(g):
                if g == 1:
                    pe.wait_ge(w_act, 2)
                    pe.wait_ge(w_dve, 2)
                for u in range(GT):
                    pe.wait_ge(xn_ready, GT * g + u + 1)
                    for c in range(KC):
                        t = pe.transpose(bank[:, XT_BANK[g % 2] + c, u * P:(u + 1) * P], xn[:, g % 2, u, c * P:(c + 1) * P],
                                         ident[:, :])
                        if u == GT - 1:
                            t.then_inc(xT_ps, 1)

            def project(g):
                pe.wait_ge(xT_act, g + 1)
                pe.wait_ge(xT_dve, g + 1)
                if g:
                    pe.wait_ge(vr_ready, g)
                    pe.wait_ge(kl_ready, g)
                for c in range(KC):
                    mm = pe.matmul(bank[0:48, 2, :], wvrkT[:, c, :], xnT[:, g % 2, c, :],
                                   start=(c == 0), stop=(c == KC - 1))
                mm.then_inc(proj_ps, 1)
                for m in range(KC):
                    if g:
                        pe.wait_ge(ql_ready, KC * (g - 1) + m + 1)
                    for c in range(KC):
                        mm = pe.matmul(bank[:, 3 + m, :], wqT[:, c, m * P:(m + 1) * P], xnT[:, g % 2, c, :],
                                       start=(c == 0), stop=(c == KC - 1))
                    mm.then_inc(proj_ps, 1)

            transpose_x(0)
            pe.wait_ge(wo_in, 16)
            for c in range(KC):
                for m in range(KC):
                    last = pe.transpose(bank[:, 7, c * D + m * P:c * D + (m + 1) * P],
                                        wo_nat[:, m, c * P:(c + 1) * P], ident[:, :])
            last.then_inc(w_ps, 1)
            pe.wait_ge(w_act, 2)
            for g in range(NG):
                if 0 < g < NG - 1:
                    transpose_x(g + 1)
                project(g)
                if g == 0:
                    transpose_x(1)
                pe.wait_ge(vr_ready, g + 1)
                if g:
                    pe.wait_ge(vl_ready, g)
                for u in range(GT):
                    t = pe.transpose(bank[:, 5, u * 32:(u + 1) * 32], vr[0:32, u * P:(u + 1) * P],
                                     ident[0:32, 0:32])
                t.then_inc(vrT_ps, 1)

            pe.wait_ge(masks, 11)
            pe.wait_ge(xT_act, NG)
            pe.wait_ge(chosen_ready, 1)
            flat = chosen[:].rearrange("p t e -> p (t e)")
            pe.matmul(bank[:, 6, 0:NT * E], below[:, :], flat, start=True, stop=True)
            pe.matmul(bank[:, 6, NT * E:2 * NT * E], ones_b[:, :], flat, start=True, stop=True).then_inc(place_ps, 1)

            def scores_for_max(b, buf, n):
                pair, qt = n // 2, n % 2
                if n == 0:
                    pe.wait_ge(q_in[buf][0], 64 * (b // 2 + 1) if isinstance(b, int) else (b - buf) * 32 + 64)
                if n == 8:
                    pe.wait_ge(q_in[buf][1], 64 * (b // 2 + 1) if isinstance(b, int) else (b - buf) * 32 + 64)
                banks = max_banks(b)
                if isinstance(b, int) and b == 0:
                    if n >= banks:
                        pe.wait_ge(max_done, n - banks + 1)
                elif n >= 2:
                    pe.wait_ge(max_done, b * 16 + (n - 1))
                elif not (isinstance(b, int) and b < 3):
                    pe.wait_ge(o_added, b * 2 - 5 + n)
                A = bank[:, n % banks, :]
                for k in range(2):
                    pe.matmul(A[:, k * S:(k + 1) * S], qs[:, buf, 2 * pair + k, qt * P:(qt + 1) * P],
                              k_all[:, bass.ds(b * S, S)], start=(k == 0), stop=True, skip_group_check=True)
                diag = A.rearrange("p (k t) -> p k t", k=2)[:, :, qt * P:(qt + 1) * P]
                pe.matmul(diag, ident_b[:, :], mask_q[:], start=False, stop=True,
                          skip_group_check=True).then_inc(p1_ps, 1)

            def transpose_max(b, buf):
                pe.wait_ge(max_done, b * 16 + 16)
                for qt in range(2):
                    t = pe.transpose(bank[0:H, 7, qt * P:(qt + 1) * P], nmax[:, buf, qt, :], ident[:, :])
                t.then_inc(mt_ps, 1)

            def scores(b, buf, q, r):
                n = 3 * q + r
                if not (isinstance(b, int) and b == 0 and n < 2):
                    pe.wait_ge(exp_done, b * 12 + (n - 1))
                A = bank[:, 2 + n % 2, :]
                if r < 2:
                    h0 = 4 * q + 2 * r
                    pe.matmul(A, ks[:, buf, 0:P], qs[:, buf, h0:h0 + 2, :], start=True, stop=True)
                    diag = A.rearrange("p (k t) -> p k t", k=2)[:, :, 0:P]
                    mm = pe.matmul(diag, ident_b[:, :], mask_k[:, 0:2, :], start=False, stop=True,
                                   skip_group_check=True)
                else:
                    pe.matmul(A, ks[:, buf, P:2 * P], qs[:, buf, 4 * q:4 * q + 4, P:2 * P],
                              start=True, stop=True)
                    mm = pe.matmul(A, ident_b[:, :], mask_k[:], start=False, stop=True, skip_group_check=True)
                mm.then_inc(s_ps, 1)

            def weigh_v(b, buf, q):
                pe.wait_ge(exp_done, b * 12 + (3 * q + 3))
                if not (isinstance(b, int) and b == 0 and q < 2):
                    pe.wait_ge(ct_ready, b * NQ + (q - 1))
                o = bank[:, 4 + q % 2, :]
                for j in range(4):
                    pe.matmul(o[32 * j:32 * j + 32, 0:S], vs[:, buf, 0, :],
                              pt[:, (3 * q + j // 2) % 6, (j % 2) * S:(j % 2 + 1) * S], start=True, stop=True)
                for j in range(4):
                    mm = pe.matmul(o[32 * j:32 * j + 32, P:S], vs[:, buf, 1, :],
                                   pt[:, (3 * q + 2) % 6, j * P:(j + 1) * P], start=False, stop=True,
                                   skip_group_check=True)
                mm.then_inc(pv_ps, 1)

            def context(b, buf, qt):
                if qt == 0:
                    pe.wait_ge(ct_ready, b * NQ + NQ)
                if isinstance(b, int) and b == 0 and qt == 0:
                    pe.wait_ge(route_ready, 1)
                else:
                    pe.wait_ge(ctx_ready, b * 2 + qt)
                for q in range(NQ):
                    t = pe.transpose(bank[:, 6, q * P:(q + 1) * P], ct[:, buf, q, qt * P:(qt + 1) * P],
                                     ident[:, :])
                t.then_inc(c_ps, 1)

            def transpose_context(b, qt):
                pe.wait_ge(ctx_ready, b * 2 + (qt + 1))
                for c in range(KC):
                    t = pe.transpose(bank[:, qt, c * P:(c + 1) * P], ctx_n[:, qt, c * P:(c + 1) * P], ident[:, :])
                t.then_inc(t_ps, 1)

            def project_out(b, qt):
                pe.wait_ge(cxt_ready, b * 2 + (qt + 1))
                for c in range(KC):
                    mm = pe.matmul(bank[:, qt, 0:D], cxt[:, qt, c, :], woT[:, c, :], start=(c == 0),
                                   stop=(c == KC - 1))
                mm.then_inc(o_ps, 1)

            def batch(b, buf, first=False, ahead=True):
                other = 1 - buf
                for s in range(12):
                    if ahead and s < 8:
                        scores_for_max(b + 1, other, 2 * s)
                    if s == 0:
                        pe.wait_ge(m_in[buf], 32 * (b // 2 + 1) if isinstance(b, int) else (b - buf) * 16 + 32)
                        pe.wait_ge(kv_ready, b * 2 + 2)
                    scores(b, buf, s // 3, s % 3)
                    if ahead and s < 8:
                        scores_for_max(b + 1, other, 2 * s + 1)
                    if s == 8 and ahead:
                        transpose_max(b + 1, other)
                    if s == 0 and not first:
                        weigh_v(b - 1, other, NQ - 1)
                    if s in (4, 7, 10):
                        weigh_v(b, buf, s // 3 - 1)
                    if not first:
                        if s == 2:
                            context(b - 1, other, 0)
                        if s == 6:
                            context(b - 1, other, 1)
                        if s in (8, 9):
                            transpose_context(b - 1, s - 8)
                        if s in (10, 11):
                            project_out(b - 1, s - 10)

            pe.wait_ge(masks, 16)
            pe.wait_ge(qs_padded, 1)
            pe.wait_ge(k_all_in, 64)
            pe.wait_ge(vl_ready, NG)
            for n in range(16):
                scores_for_max(0, 0, n)
            pe.wait_ge(xT_dve, NG)
            transpose_max(0, 0)
            pe.wait_ge(qs_padded, 2)
            batch(0, 0, first=True)
            pe.wait_ge(k_all_in, 128)
            batch(1, 1)
            with pe.Fori(1, B // 2 - 1) as i:
                batch(i * 2, 0)
                batch(i * 2 + 1, 1)
            batch(B - 2, 0)
            batch(B - 1, 1, ahead=False)

            pe.wait_ge(experts_in, 16 * N_EXP)
            pe.wait_ge(tile_e_ready, 1)

            def tile_xT(j, r, came):
                pe.wait_ge(gathered[r], came)
                for c in range(KC):
                    t = pe.transpose(bank[:, 7, c * P:(c + 1) * P], xg[:, r, c * P:(c + 1) * P], ident[:, :])
                t.then_inc(xgT_ps, 1)

            def expert(j):
                return pe.value_load(tile_e[0:1, bass.ds(j, 1)], min_val=0, max_val=E - 1)

            def tile_gate_up(j, buf, e):
                pe.wait_ge(xgT_ready, j + 1)
                for c in range(KC):
                    mm = pe.matmul(bank[:, 2 + buf, :], xT[:, buf, c, :],
                                   wgu[:, bass.ds(e * KC + c, 1), :], start=(c == 0), stop=(c == KC - 1))
                mm.then_inc(gu_ps, 1)

            def tile_hT(j, buf):
                pe.wait_ge(h_ready, j + 1)
                for c in range(FC):
                    t = pe.transpose(bank[:, 6, c * P:(c + 1) * P], hh[:, buf, c * P:(c + 1) * P], ident[:, :])
                t.then_inc(hT_ps, 1)

            def tile_down(j, buf, e):
                pe.wait_ge(hT_ready, j + 1)
                for c in range(FC):
                    mm = pe.matmul(bank[:, 4 + buf, 0:D], hT[:, buf, c, :],
                                   wdn[:, bass.ds(e * FC + c, 1), :], start=(c == 0), stop=(c == FC - 1))
                mm.then_inc(dn_ps, 1)

            def tiles(base, turn, first):
                es = {}
                for u in range(RING):
                    j = base + u
                    es[u] = expert(j)
                    tile_gate_up(j, u % 2, es[u])
                    if not (first and u < 2) and u < 2:
                        es[u - 2] = expert(j - 2)
                    tile_xT(j + 1, (u + 1) % RING, turn * 16 + (32 if u == RING - 1 else 16))
                    if not (first and u < 2):
                        tile_down(j - 2, u % 2, es[u - 2])
                    if first:
                        last_output(u)
                    if not (first and u == 0):
                        tile_hT(j - 1, (u + 1) % 2)

            def last_output(u):
                if u == 0:
                    context(B - 1, 1, 0)
                if u == 1:
                    transpose_context(B - 1, 0)
                    context(B - 1, 1, 1)
                    project_out(B - 1, 0)
                    pe.wait_ge(ctx_ready, 2 * B)
                if u == 2:
                    transpose_context(B - 1, 1)
                    project_out(B - 1, 1)

            tile_xT(0, 0, 16)
            weigh_v(B - 1, 1, NQ - 1)
            tiles(0, 0, True)
            with pe.Fori(1, MT // RING) as i:
                tiles(i * RING, i, False)
            e0, e1 = expert(MT - 2), expert(MT - 1)
            pe.wait_ge(y_ready, MT - 3)
            tile_down(MT - 2, 0, e0)
            tile_hT(MT - 1, 1)
            pe.wait_ge(y_ready, MT - 2)
            tile_down(MT - 1, 1, e1)

        @block.scalar
        def _(act):
            def root(n, ts):
                act.wait_ge(var_ready, n + 1)
                act.activation(std0[:, ts], var_e[:, ts], ACT.Sqrt).then_inc(std_ready, 1)

            root(0, LN_PARTS[0])
            act.wait_ge(w_ps, 2)
            act.activation(wqT[:].rearrange("p c e -> p (c e)"), bank[:, 6, :], ACT.Copy,
                           scale=QSCALE).then_inc(w_act, 1)
            act.activation(wvrkT[:].rearrange("p c e -> p (c e)"), bank[:, 5, 0:KC * 48],
                           ACT.Copy).then_inc(w_act, 1)

            def keep_xT(g):
                act.wait_ge(xT_ps, 2 * g + 1)
                if g >= 2:
                    act.wait_ge(proj_ps, 3 * (g - 1))
                act.activation(xnT[:, g % 2, 0, :], bank[:, XT_BANK[g % 2], :], ACT.Copy).then_inc(xT_act, 1)

            keep_xT(0)
            root(1, LN_PARTS[1])
            act.wait_ge(b_in, 64)
            for g in range(NG):
                if 0 < g < NG - 1:
                    keep_xT(g + 1)
                act.wait_ge(proj_ps, 3 * g + 1)
                if g:
                    act.wait_ge(vrT_ps, g)
                act.activation(vr[0:32, :], bank[0:32, 2, :], ACT.Identity, bias=bvrk[0:32, :]
                               ).then_inc(vr_ready, 1)
                if g:
                    act.wait_ge(k_stored, 32 * g)
                act.activation(khl[32:48, 0, :], bank[32:48, 2, :], ACT.Identity, bias=bvrk[32:48, :]
                               ).then_inc(kh_ready, 1)
                if g:
                    act.wait_ge(q_stored, 32 * g)
                else:
                    act.wait_ge(w_ps, 2)
                    act.wait_ge(w_dve, 1)
                for m in range(KC):
                    act.wait_ge(proj_ps, 3 * g + 2 + m)
                    act.activation(qhl[:, 0, m, :], bank[:, 3 + m, :], ACT.Identity, bias=bq_s[:, m:m + 1]
                                   ).then_inc(qh_ready, 1)
                if g == 0:
                    keep_xT(1)

            act.wait_ge(shifted, 1)
            act.activation(probs[:], logits[:], ACT.Exp).then_inc(exped, 1)

            def exp_scores(b, n):
                act.wait_ge(s_ps, b * 12 + (n + 1))
                if not (isinstance(b, int) and b == 0 and n < 6):
                    act.wait_ge(pv_ps, b * NQ + (n // 3 - 1))
                act.activation(pt[:, n % 6, :], bank[:, 2 + n % 2, :], ACT.Exp).then_inc(exp_done, 1)

            def keep_context(b, buf, q):
                act.wait_ge(pv_ps, b * NQ + (q + 1))
                if not (isinstance(b, int) and b < 2):
                    act.wait_ge(c_ps, b * 2 - 2)
                act.activation(ct[:, buf, q, :], bank[:, 4 + q % 2, 0:S], ACT.Copy).then_inc(ct_ready, 1)

            def keep_cxt(b, qt):
                act.wait_ge(t_ps, b * 2 + (qt + 1))
                act.activation(cxt[:, qt].rearrange("p c t -> p (c t)"), bank[:, qt, 0:D], ACT.Copy
                               ).then_inc(cxt_ready, 1)

            def keep_max(b, buf):
                act.wait_ge(mt_ps, b + 1)
                act.activation(mt[:, buf, 0, :], bank[0:H, 7, 0:S], ACT.Copy).then_inc(mth_ready, 1)

            def load_experts(n):
                c4, which = n // 3, n % 3
                es = slice(c4 * E // 4, (c4 + 1) * E // 4)
                gs = slice(es.start * KC, es.stop * KC)
                src = (wgate, wup, wdown)[which][es].rearrange("e (c p) f -> p (e c) f", p=P)
                dst = wdn[:, gs, :] if which == 2 else wgu[:, gs, which * F:(which + 1) * F]
                act.dma_start(dst, src).then_inc(experts_in, 16)

            def batch(b, buf, first=False, ahead=True):
                other = 1 - buf
                for s in range(12):
                    exp_scores(b, s)
                    if isinstance(b, int) and b < 2 and s % 2:
                        load_experts(b * N_EXP // 2 + s // 2)
                    if s == 0 and not first:
                        keep_context(b - 1, other, NQ - 1)
                    if s in (4, 7, 10):
                        keep_context(b, buf, s // 3 - 1)
                    if s == 8 and ahead:
                        keep_max(b + 1, other)
                    if s in (9, 10) and not first:
                        keep_cxt(b - 1, s - 9)

            keep_max(0, 0)
            batch(0, 0, first=True)
            batch(1, 1)
            with act.Fori(1, B // 2 - 1) as i:
                batch(i * 2, 0)
                batch(i * 2 + 1, 1)
            batch(B - 2, 0)
            batch(B - 1, 1, ahead=False)
            def tile_silu(j, buf):
                act.wait_ge(gu_ps, j + 1)
                act.activation(sg[:, buf, :], bank[:, 2 + buf, 0:F], ACT.Silu).then_inc(silu_ready, 1)

            def tile_xT(j, buf):
                act.wait_ge(xgT_ps, j + 1)
                act.activation(xT[:, buf].rearrange("p c t -> p (c t)"), bank[:, 7, 0:D], ACT.Copy
                               ).then_inc(xgT_ready, 1)

            def tile_y(j, r, sent):
                act.wait_ge(dn_ps, j + 1)
                if sent is not None:
                    act.wait_ge(y_sent[r], sent)
                act.activation(ys[:, r, :], bank[:, 4 + r % 2, 0:D], ACT.Copy).then_inc(y_ready, 1)

            def tiles(base, turn, first):
                for u in range(RING):
                    j = base + u
                    tile_silu(j, u % 2)
                    tile_xT(j + 1, (u + 1) % 2)
                    if first and 1 <= u < 3:
                        keep_cxt(B - 1, u - 1)
                    if u < 2 and not first:
                        tile_y(j - 2, u + 2, None if isinstance(turn, int) and turn == 1 else turn * 16 - 16)
                    elif u >= 2:
                        tile_y(j - 2, u - 2, None if first else turn * 16)

            tile_xT(0, 0)
            keep_context(B - 1, 1, NQ - 1)
            tiles(0, 0, True)
            tiles(RING, 1, False)
            with act.Fori(2, MT // RING) as i:
                tiles(i * RING, i, False)
            for u in range(2):
                tile_y(MT - 2 + u, RING - 2 + u, 16 * (MT // RING - 1))

            for r in range(RING):
                act.wait_ge(y_sent[r], 16 * (MT // RING))
            for t in range(1, NT, 2):
                load_y(act, t)

        @block.vector
        def _(dve):
            ln = Steps(dve, dve_ln)

            def statistics(n, ts):
                for t in range(ts.start, ts.stop):
                    dve.wait_ge(x_in[t // GT], 16)
                    last = dve.bn_stats(stats[:, t, :], xs[:, t, :])
                ln(last)
                for t in range(ts.start, ts.stop):
                    last = dve.bn_aggr(mv[:, t, :], stats[:, t, :])
                ln(last)
                dve.tensor_scalar(var_e[:, ts], mv[:, ts, 1], LN_EPS, None, ALU.add).then_inc(var_ready, 1)
                dve.wait_ge(std_ready, n + 1)
                ln(dve.reciprocal(rstd[:, ts], std0[:, ts]))
                ln(dve.tensor_tensor(rstd[:, ts], rstd[:, ts], var_e[:, ts], ALU.mult))
                ln(dve.tensor_tensor(rstd[:, ts], rstd[:, ts], std0[:, ts], ALU.add))
                ln(dve.tensor_scalar(rstd[:, ts], rstd[:, ts], 0.5, None, ALU.mult))
                ln(dve.reciprocal(rstd[:, ts], rstd[:, ts]))

            def normalise(g):
                if g >= 2:
                    dve.wait_ge(xT_ps, 2 * (g - 1))
                    dve.wait_ge(xn_stored[g % 2], 16 * (g // 2))
                for u in range(GT):
                    t = g * GT + u
                    dve.tensor_scalar(xn[:, g % 2, u, :], xs[:, t, :], mv[:, t, 0:1], rstd[:, t:t + 1],
                                      ALU.subtract, ALU.mult).then_inc(xn_ready, 1)

            def keep_xT(g):
                dve.wait_ge(xT_ps, 2 * g + 2)
                if g >= 2:
                    dve.wait_ge(proj_ps, 3 * (g - 1))
                dve.tensor_copy(xnT[:, g % 2, 1, :], bank[:, XT_BANK[g % 2] + 1, :]).then_inc(xT_dve, 1)

            statistics(0, LN_PARTS[0])
            normalise(0)
            keep_xT(0)
            dve.wait_ge(b_in, 64)
            dve.tensor_scalar(bq_s[:, :], bq[:, :], QSCALE, None, ALU.mult).then_inc(w_dve, 1)
            dve.wait_ge(w_ps, 3)
            dve.tensor_copy(woT[:].rearrange("p c e -> p (c e)"), bank[:, 7, :]).then_inc(w_dve, 1)
            dve.wait_ge(w_dve, 2)
            statistics(1, LN_PARTS[1])
            normalise(1)
            dve.wait_ge(masks, 15)
            for g in range(NG):
                if 0 < g < NG - 1:
                    keep_xT(g + 1)
                dve.wait_ge(kh_ready, g + 1)
                dve.scalar_tensor_tensor(out=khl[32:48, 1, :], in0=bank[32:48, 2, :], scalar=bvrk[32:48, :],
                                         in1=khl[32:48, 0, :].bitcast(F32), op0=ALU.add, op1=ALU.subtract
                                         ).then_inc(kl_ready, 1)
                for m in range(KC):
                    dve.wait_ge(qh_ready, KC * g + m + 1)
                    dve.scalar_tensor_tensor(out=qhl[:, 1, m, :], in0=bank[:, 3 + m, :],
                                             scalar=bq_s[:, m:m + 1], in1=qhl[:, 0, m, :].bitcast(F32),
                                             op0=ALU.add, op1=ALU.subtract).then_inc(ql_ready, 1)
                if g == 0:
                    keep_xT(1)
                if g < NG - 2:
                    normalise(g + 2)
                dve.wait_ge(vrT_ps, g + 1)
                vl = bank[:, 5, 0:GT * 32].rearrange("p (u c) -> p u c", u=GT)
                dve.tensor_copy(v_all[:, g * GT:(g + 1) * GT, 0:HD], vl[:, :, 0:HD])
                dve.tensor_copy(logits[:, g * GT:(g + 1) * GT, :], vl[:, :, HD:HD + E]).then_inc(vl_ready, 1)

            rt = Steps(dve, dve_rt)
            dve.wait_ge(vl_ready, NG)

            def over_e(ap):
                return ap.unsqueeze(2).to_broadcast([P, NT, E])

            rt(dve.tensor_reduce(rowstat[:, :], logits[:], AX.X, ALU.max))
            dve.tensor_tensor(logits[:], logits[:], over_e(rowstat[:, :]), ALU.subtract).then_inc(shifted, 1)
            dve.wait_ge(exped, 1)
            rt(dve.tensor_reduce(rowstat[:, :], probs[:], AX.X, ALU.add))
            rt(dve.reciprocal(rowstat[:, :], rowstat[:, :]))
            rt(dve.tensor_tensor(probs[:], probs[:], over_e(rowstat[:, :]), ALU.mult))
            for t in range(NT):
                last = dve.max(top_w[:, t, :], probs[:, t, :])
            rt(last)
            for t in range(NT):
                last = dve.max_index(top_e[:, t, :], top_w[:, t, :], probs[:, t, :])
            rt(last)
            dve.wait_ge(masks, 21)
            rt(dve.tensor_reduce(rowstat[:, :], top_w[:, :, 0:TOP_K], AX.X, ALU.add))
            rt(dve.reciprocal(rowstat[:, :], rowstat[:, :]))
            rt(dve.tensor_tensor(row_coef[:, :, :, 1].bitcast(F32), top_w[:, :, 0:TOP_K],
                                 rowstat[:, :].unsqueeze(2).to_broadcast([P, NT, TOP_K]), ALU.mult))
            rt(dve.tensor_copy(top_ef[:], top_e[:, :, 0:TOP_K]))
            choice = onehot.rearrange("p t k e -> p (t k) e")
            rt(dve.tensor_tensor(choice, top_ef[:].rearrange("p t k -> p (t k)").unsqueeze(2).to_broadcast([P, NT * TOP_K, E]),
                                 iota_e[:].unsqueeze(1).to_broadcast([P, NT * TOP_K, E]), ALU.is_equal))
            with nc.allow_low_precision(reason="each sum is 0 or 1"):
                dve.tensor_reduce(chosen[:], onehot.rearrange("p t k e -> p t e k"), AX.X, ALU.add
                                  ).then_inc(chosen_ready, 1)
            scanned_t = scan_t[:, (NT.bit_length() - 1) % 2]
            scanned_e = scan_e[:, (E.bit_length() - 1) % 2]
            count = scanned_t[:, PADT + NT - 1, :]
            before = scanned_t[:, PADT - 1:PADT + NT - 1, :]
            end = scanned_e[:, PADE:]

            def sum_over_tiles():
                dve.wait_ge(place_ps, 1)
                rt(dve.tensor_copy(scan_t[:, 0, PADT:, :], bank[:, 6, NT * E:2 * NT * E].rearrange("p (t e) -> p t e", t=NT)))
                src, step = 0, 1
                while step < NT:
                    rt(dve.tensor_tensor(scan_t[:, 1 - src, PADT:, :], scan_t[:, src, PADT:, :],
                                         scan_t[:, src, PADT - step:PADT + NT - step, :], ALU.add))
                    src, step = 1 - src, 2 * step

            def first_rows():
                rt(dve.tensor_scalar(ntile_i[:, :], count, float(P - 1), None, ALU.add))
                rt(dve.tensor_scalar(ntile_i[:, :], ntile_i[:, :], P.bit_length() - 1, None,
                                     ALU.logical_shift_right))
                rt(dve.tensor_copy(scan_e[:, 0, PADE:], ntile_i[:, :]))
                esrc, step = 0, 1
                while step < E:
                    rt(dve.tensor_tensor(scan_e[:, 1 - esrc, PADE:], scan_e[:, esrc, PADE:],
                                         scan_e[:, esrc, PADE - step:PADE + E - step], ALU.add))
                    esrc, step = 1 - esrc, 2 * step
                rt(dve.tensor_tensor(first_row[:, :], end, ntile_i[:, :], ALU.subtract))
                rt(dve.tensor_scalar(first_row[:, :], first_row[:, :], float(P), None, ALU.mult))

            def choice_slots():
                rt(dve.tensor_tensor(probs[:], before, bank[:, 6, 0:NT * E].rearrange("p (t e) -> p t e", t=NT),
                                     ALU.add))
                rt(dve.tensor_tensor(probs[:], probs[:], first_row[:].unsqueeze(1).to_broadcast([P, NT, E]),
                                     ALU.add))
                for k in range(TOP_K):
                    last = dve.tensor_tensor(onehot[:, :, k, :], onehot[:, :, k, :], probs[:], ALU.mult)
                rt(last)
                rt(dve.tensor_reduce(slot_f[:].rearrange("p t k -> p (t k)"), choice, AX.X, ALU.add))

            def slot_numbers():
                rt(dve.tensor_copy(slot_i[:], slot_f[:]))
                rt(dve.tensor_scalar(slot_p[:], slot_i[:], P - 1, None, ALU.bitwise_and))
                rt(dve.tensor_scalar(slot_i[:], slot_i[:], P.bit_length() - 1, None, ALU.logical_shift_right))
                rt(dve.tensor_copy(slot_pf[:], slot_p[:]))
                rt(dve.tensor_copy(slot_f[:], slot_i[:]))
                rt(dve.scalar_tensor_tensor(out=slot_f[:], in0=slot_pf[:], scalar=float(MT), in1=slot_f[:],
                                            op0=ALU.mult, op1=ALU.add))
                dve.tensor_copy(slot_i[:], slot_f[:]).then_inc(route_ready, 1)

            def tile_experts():
                rt(dve.tensor_tensor(tile_ge, tile_no[:].unsqueeze(2).to_broadcast([1, MT, E]),
                                     end[0:1].unsqueeze(1).to_broadcast([1, MT, E]), ALU.is_ge))
                rt(dve.tensor_reduce(tile_ef[:], tile_ge, AX.X, ALU.add))
                dve.tensor_scalar(tile_e[:], tile_ef[:], float(E - 1), None, ALU.min).then_inc(tile_e_ready, 1)

            def row_max(b, buf, n):
                pair, qt = n // 2, n % 2
                dve.wait_ge(p1_ps, b * 16 + (n + 1))
                A = bank[:, n % max_banks(b), :].rearrange("p (k t) -> p k t", k=2)
                dve.tensor_reduce(nmax[:, buf, qt, 2 * pair:2 * pair + 2], A[:, :, 0:(qt + 1) * P], AX.X, ALU.max,
                                  negate=True).then_inc(max_done, 1)

            def split_max(b, buf):
                dve.wait_ge(mth_ready, b + 1)
                dve.tensor_tensor(mt[:, buf, 1, :], bank[0:H, 7, 0:S], mt[:, buf, 0, :].bitcast(F32),
                                  ALU.subtract).then_inc(mtl_ready, 1)

            def normalise_context(b, qt):
                dve.wait_ge(c_ps, b * 2 + (qt + 1))
                c = bank[:, 6, :].rearrange("p (h v) -> p h v", h=H)
                dve.reciprocal(rden[:, qt, :], c[:, :, HD]).then_inc(rden_ready, 1)
                dve.wait_ge(rden_ready, b * 2 + (qt + 1))
                dve.tensor_tensor(ctx_n[:, qt].rearrange("p (h v) -> p h v", h=H), c[:, :, 0:HD],
                                  rden[:, qt, :].unsqueeze(2).to_broadcast([P, H, HD]), ALU.mult
                                  ).then_inc(ctx_ready, 1)

            def add_out(b, qt):
                dve.wait_ge(o_ps, b * 2 + (qt + 1))
                tile = xs[:, bass.ds(b * 2 + qt, 1), :].rearrange("p a d -> p (a d)")
                dve.tensor_tensor(tile, tile, bank[:, qt, 0:D], ALU.add).then_inc(o_added, 1)

            def batch(b, buf, first=False, ahead=True):
                other = 1 - buf
                for s in range(8):
                    if ahead:
                        row_max(b + 1, other, 2 * s)
                        row_max(b + 1, other, 2 * s + 1)
                    if s in (2, 6) and not first:
                        normalise_context(b - 1, s // 4)
                    if first:
                        if s == 1:
                            sum_over_tiles()
                        if s == 3:
                            first_rows()
                        if s == 5:
                            choice_slots()
                    elif not ahead and s == 4:
                        dve.wait_ge(list_in, 16)
                        dve.tensor_scalar(get_row[:, :], slots[:, :, 0], T - 1, None, ALU.bitwise_and
                                          ).then_inc(rows_ready, 1)
                    elif isinstance(b, int) and b == 1:
                        if s == 0:
                            slot_numbers()
                        if s == 4:
                            tile_experts()
                if ahead:
                    split_max(b + 1, other)
                if not first:
                    for qt in range(2):
                        add_out(b - 1, qt)

            for n in range(16):
                row_max(0, 0, n)
            split_max(0, 0)
            dve.wait_ge(xb_ready, NT)
            batch(0, 0, first=True)
            batch(1, 1)
            with dve.Fori(1, B // 2 - 1) as i:
                batch(i * 2, 0)
                batch(i * 2 + 1, 1)
            batch(B - 2, 0)
            batch(B - 1, 1, ahead=False)

            def tile_h(j, buf):
                dve.wait_ge(silu_ready, j + 1)
                dve.scalar_tensor_tensor(out=hh[:, buf, :], in0=sg[:, buf, :],
                                         scalar=slots[:, bass.ds(j, 1), 1].bitcast(F32),
                                         in1=bank[:, 2 + buf, F:2 * F], op0=ALU.mult, op1=ALU.mult
                                         ).then_inc(h_ready, 1)

            def tile_hT(j, buf):
                dve.wait_ge(hT_ps, j + 1)
                dve.tensor_copy(hT[:, buf].rearrange("p c t -> p (c t)"), bank[:, 6, 0:F]).then_inc(hT_ready, 1)

            def tiles(base, first):
                for u in range(RING):
                    tile_h(base + u, u % 2)
                    if first:
                        if u < 2:
                            normalise_context(B - 1, u)
                        if 1 <= u < 3:
                            add_out(B - 1, u - 1)
                    if not (first and u == 0):
                        tile_hT(base + u - 1, (u + 1) % 2)

            tiles(0, True)
            with dve.Fori(1, MT // RING) as i:
                tiles(i * RING, False)
            tile_hT(MT - 1, 1)

            for t in range(NT):
                dve.wait_ge(y_in[t], 16)
                dve.tensor_tensor(yc[:, t, 0:2], yc[:, t, 0:2], yc[:, t, 2:4], ALU.add).then_inc(combined, 1)
                dve.wait_ge(combined, 2 * t + 1)
                dve.tensor_tensor(yc[:, t, 0], yc[:, t, 0], yc[:, t, 1], ALU.add).then_inc(combined, 1)
                dve.wait_ge(combined, 2 * t + 2)
                dve.tensor_tensor(xs[:, t, :], xs[:, t, :], yc[:, t, 0], ALU.add).then_inc(added, 1)


_INS = ['L0_attn_x', 'L0_attn_Wqkv_w', 'L0_attn_Wqkv_b', 'L0_attn_out_w', 'L0_attn_out_b',
        'L0_ffn_w_router', 'L0_ffn_w_gate', 'L0_ffn_w_up', 'L0_ffn_w_down']
_OUTS = [((8, 256, 256), 'float32')]


def kernel(**inputs):
    import numpy as _np
    import concourse.bacc as _bacc
    from concourse import mybir as _mybir
    from concourse.bass_utils import run_bass_kernel_spmd as _run

    nc = _bacc.Bacc("TRN2", target_bir_lowering=False, num_devices=1)
    arrays, args = {}, []
    for name in _INS:
        a = _np.ascontiguousarray(inputs[name])
        arrays[f"in_{name}_dram"] = a
        args.append(nc.dram_tensor(f"in_{name}_dram", a.shape, _mybir.dt.from_np(a.dtype), kind="ExternalInput").ap())
    for i, (shape, dtype) in enumerate(_OUTS):
        dt = _mybir.dt.from_np(_np.dtype(dtype))
        args.append(nc.dram_tensor(f"out_{i}_dram", shape, dt, kind="ExternalOutput").ap())
    attention_and_experts(nc, *args)
    r = _run(nc, [arrays], core_ids=[0])
    return r.results[0]["out_0_dram"]
```

```python
from contextlib import ExitStack

import concourse.bass as bass
from concourse import mybir

ALU = mybir.AluOpType
ACT = mybir.ActivationFunctionType
AX = mybir.AxisListType
F32 = mybir.dt.float32
F32R = mybir.dt.float32r
BF16 = mybir.dt.bfloat16
I32 = mybir.dt.int32
U32 = mybir.dt.uint32

P = 128
TOP_K = 4
LN_EPS = 1e-5
MASKED = -1e30


class Steps:

    def __init__(self, eng, sem):
        self.eng, self.sem, self.n = eng, sem, 0

    def __call__(self, ins):
        self.n += 1
        ins.then_inc(self.sem, 1)
        self.eng.wait_ge(self.sem, self.n)


def attention_and_experts(nc, x, wqkv, bqkv, wout, bout, wrouter, wgate, wup, wdown, out):
    B, S, D = x.shape
    E, _, F = wgate.shape
    T = B * S
    NT = T // P
    HD = (wqkv.shape[0] - D) // 2
    H = D // HD
    KC = D // P
    FC = F // P
    GT = 4
    NG = NT // GT
    GW = GT * P
    NQ = H // 4
    RING = 4
    MT = (T * TOP_K + E * (P - 1)) // P
    TURNS, REST = MT // RING, MT % RING
    NOROW = T
    assert (D, S, F, HD, E, KC, FC) == (2 * P, 2 * P, 2 * P, 16, 16, 2, 2) and T & (T - 1) == 0
    VW = 32
    QSCALE = float(HD) ** -0.5

    x_rows = x.rearrange("b s d -> (b s) d")
    out_rows = out.rearrange("b s d -> (b s) d")

    xn_d = nc.dram_tensor("xn_d", (T, D), F32).ap()
    q_d = nc.dram_tensor("q_d", (2, D, T), F32).ap()
    k_d = nc.dram_tensor("k_d", (2, HD, T), F32).ap()
    slots_d = nc.dram_tensor("slots_d", (P * MT, 2), I32).ap()

    with ExitStack() as ctx:
        def sb(name, shape, dt=F32):
            return ctx.enter_context(nc.sbuf_tensor(name, shape, dt))

        def sem(name):
            return ctx.enter_context(nc.semaphore(name))

        bank = ctx.enter_context(nc.psum_tensor("bank", [P, 8, 512], F32))

        wgu = sb("wgu", [P, E * KC, 2 * F])
        wdn = sb("wdn", [P, E * FC, D])
        xs = sb("xs", [P, NT, D])
        k_all = sb("k_all", [P, T], F32R)
        ks = sb("ks", [P, 2, S], F32R)
        v_all = sb("v_all", [P, NT, VW])
        vs = sb("vs", [P, 2, 2, VW])
        pt = sb("pt", [P, 6, 512])
        ct = sb("ct", [P, 2, NQ, S])
        out_buf = sb("out_buf", [P, 4 * D])
        ctx_n = out_buf[:, 0:2 * D].rearrange("p (a d) -> p a d", a=2)
        cxt = out_buf[:, 2 * D:].rearrange("p (a c t) -> p a c t", a=2, c=KC)
        rden = sb("rden", [P, 2, H])
        nmax = sb("nmax", [P, 2, 2, H])
        mt = sb("mt", [H, 2, 2, S], F32R)
        ident = sb("ident", [P, P])
        ident_b = sb("ident_b", [P, P], BF16)
        below = sb("below", [P, P], BF16)
        ones_b = sb("ones_b", [P, P], BF16)
        mask_q = sb("mask_q", [P, 2, P], BF16)
        mask_k = sb("mask_k", [P, 4, P], BF16)
        wqT = sb("wqT", [P, KC, D])
        wvrkT = sb("wvrkT", [P, KC, 48])
        woT = sb("woT", [P, KC, D])
        bq = sb("bq", [P, KC])
        bq_s = sb("bq_s", [P, KC])
        bvrk = sb("bvrk", [48, 1])
        bo = sb("bo", [P, D])
        stats = sb("stats", [P, NT, 6])
        mv = sb("mv", [P, NT, 2])
        var_e = sb("var_e", [P, NT])
        std0 = sb("std0", [P, NT])
        rstd = sb("rstd", [P, NT])
        logits = sb("logits", [P, NT, E])
        probs = sb("probs", [P, NT, E])
        rowstat = sb("rowstat", [P, NT])
        top_w = sb("top_w", [P, NT, 8])
        top_e = sb("top_e", [P, NT, 8], U32)
        top_ef = sb("top_ef", [P, NT, TOP_K])
        iota_e = sb("iota_e", [P, E])
        onehot = out_buf[:].rearrange("p (t k e) -> p t k e", t=NT, k=TOP_K)
        chosen = sb("chosen", [P, NT, E], BF16)
        PADT = NT // 2
        scan_t = sb("scan_t", [P, 2, PADT + NT, E])
        PADE = E // 2
        scan_e = sb("scan_e", [P, 2, PADE + E])
        ntile_i = sb("ntile_i", [P, E], I32)
        first_row = sb("first_row", [P, E])
        slot_i = sb("slot_i", [P, NT, TOP_K], I32)
        slot_p = sb("slot_p", [P, NT, TOP_K], I32)
        slot_f = sb("slot_f", [P, NT, TOP_K])
        slot_pf = sb("slot_pf", [P, NT, TOP_K])
        row_coef = sb("row_coef", [P, NT, TOP_K, 2], I32)
        tile_no = sb("tile_no", [1, MT])
        tile_ge = scan_t[0:1].rearrange("p a t e -> p (a t e)").bitcast(BF16)[:, 0:MT * E].rearrange("p (j e) -> p j e", j=MT)
        tile_ef = sb("tile_ef", [1, MT])
        tile_e = sb("tile_e", [1, MT], I32)
        scat_to = sb("scat_to", [P, 2, TOP_K], I32)
        scat_val = sb("scat_val", [P, 2, TOP_K, 2], I32)
        slots = sb("slots", [P, MT + RING, 2], I32)
        get_row = sb("get_row", [P, MT + RING], I32)
        get_now = sb("get_now", [P, RING], I32)
        put_now = sb("put_now", [P, RING], I32)

        WORK = 32 * 256
        with nc.sbuf_tensor("early", [P, WORK], F32) as early:
            pass
        with nc.sbuf_tensor("qs", [P, 2, H, S], F32R) as qs:
            pass
        late = sb("late", [P, WORK])

        def carve(region, spans, at=0):
            found = []
            for n in spans:
                found.append(region[:, at:at + n])
                at += n
            assert at <= WORK
            return found

        v_xn, v_xnT, v_qhl, v_khl, v_vr, v_wo = carve(
            early, [2 * GT * D, 2 * KC * GW, 2 * KC * GW, 2 * GW, GW, KC * D])
        xn = v_xn.rearrange("p (b u d) -> p b u d", b=2, u=GT)
        xnT = v_xnT.rearrange("p (b c t) -> p b c t", b=2, c=KC)
        qhl = v_qhl.bitcast(F32R).rearrange("p (a m t) -> p a m t", a=2, m=KC)
        khl = v_khl.bitcast(F32R).rearrange("p (a t) -> p a t", a=2)
        vr = v_vr
        v_wn, = carve(early, [KC * D + D], at=2 * GT * D + 2 * KC * GW)
        wq_nat = v_wn[:, 0:KC * D].rearrange("p (m d) -> p m d", m=KC)
        wvrk_nat = v_wn[:, KC * D:KC * D + D]
        wo_nat = v_wo.rearrange("p (m d) -> p m d", m=KC)
        v_xg, v_xT, v_s, v_h, v_hT, v_y = carve(late, [RING * D, 2 * D, 2 * F, 2 * F, 2 * F, RING * D])
        assert (2 * RING * D + 2 * D + 6 * F) * 2 <= WORK
        xg = v_xg.rearrange("p (r d) -> p r d", r=RING)
        xT = v_xT.rearrange("p (b c t) -> p b c t", b=2, c=KC)
        sg = v_s.rearrange("p (b f) -> p b f", b=2)
        hh = v_h.rearrange("p (b f) -> p b f", b=2)
        hT = v_hT.rearrange("p (b c t) -> p b c t", b=2, c=FC)
        ys = v_y.rearrange("p (r d) -> p r d", r=RING)

        x_in = [sem(f"x_in{g}") for g in range(NG)]
        w_in = sem("w_in")
        b_in = sem("b_in")
        wo_in = sem("wo_in")
        bo_in = sem("bo_in")
        experts_in = sem("experts_in")
        masks = sem("masks")
        consts = sem("consts")
        w_ps = sem("w_ps")
        w_act = sem("w_act")
        w_dve = sem("w_dve")
        var_ready = sem("var_ready")
        std_ready = sem("std_ready")
        dve_ln = sem("dve_ln")
        xn_ready = sem("xn_ready")
        xb_ready = sem("xb_ready")
        xn_stored = [sem(f"xn_stored{b}") for b in range(2)]
        xT_ps = sem("xT_ps")
        xT_act = sem("xT_act")
        xT_dve = sem("xT_dve")
        proj_ps = sem("proj_ps")
        vr_ready = sem("vr_ready")
        kh_ready = sem("kh_ready")
        kl_ready = sem("kl_ready")
        qh_ready = sem("qh_ready")
        ql_ready = sem("ql_ready")
        q_stored = sem("q_stored")
        k_stored = sem("k_stored")
        vrT_ps = sem("vrT_ps")
        vl_ready = sem("vl_ready")
        k_all_in = sem("k_all_in")
        dve_rt = sem("dve_rt")
        shifted = sem("shifted")
        exped = sem("exped")
        chosen_ready = sem("chosen_ready")
        place_ps = sem("place_ps")
        route_ready = sem("route_ready")
        tile_e_ready = sem("tile_e_ready")
        list_init = sem("list_init")
        init_stored = sem("init_stored")
        scat_copied = sem("scat_copied")
        scattered = [sem(f"scattered{b}") for b in range(2)]
        list_in = sem("list_in")
        rows_ready = sem("rows_ready")
        q_in = [[sem(f"q_in{b}{h}") for h in range(2)] for b in range(2)]
        kv_ready = sem("kv_ready")
        qs_padded = sem("qs_padded")
        p1_ps = sem("p1_ps")
        max_done = sem("max_done")
        mt_ps = sem("mt_ps")
        mth_ready = sem("mth_ready")
        mtl_ready = sem("mtl_ready")
        m_in = [sem(f"m_in{b}") for b in range(2)]
        s_ps = sem("s_ps")
        exp_done = sem("exp_done")
        pv_ps = sem("pv_ps")
        ct_ready = sem("ct_ready")
        c_ps = sem("c_ps")
        rden_ready = sem("rden_ready")
        ctx_ready = sem("ctx_ready")
        t_ps = sem("t_ps")
        cxt_ready = sem("cxt_ready")
        o_ps = sem("o_ps")
        o_added = sem("o_added")
        now_ready = sem("now_ready")
        pool_gate = sem("pool_gate")
        put_ready = sem("put_ready")
        gathered = [sem(f"gathered{r}") for r in range(RING)]
        y_sent = [sem(f"y_sent{r}") for r in range(RING)]
        xgT_ps = sem("xgT_ps")
        xgT_ready = sem("xgT_ready")
        gu_ps = sem("gu_ps")
        silu_ready = sem("silu_ready")
        h_ready = sem("h_ready")
        hT_ps = sem("hT_ps")
        hT_ready = sem("hT_ready")
        dn_ps = sem("dn_ps")
        y_ready = sem("y_ready")
        base_stored = sem("base_stored")

        XT_BANK = [0, 6]
        CHOICE_PARTS = [(0, 1), (1, 3), (3, 4)]
        N_W = 4
        N_EXP = 3 * B

        block = ctx.enter_context(nc.Block())

        def tiles_on(r):
            return TURNS + (r < REST)

        def max_banks(b):
            return 6 if isinstance(b, int) and b == 0 else 2


        @block.sync
        def _(sp):
            def load_x(g):
                sp.dma_start(xs[:, g * GT:(g + 1) * GT, :],
                             x_rows[g * GW:(g + 1) * GW, :].rearrange("(u p) d -> p u d", p=P)
                             ).then_inc(x_in[g], 16)

            def column(bias):
                return bias.rearrange("(p a) -> p a", a=1)

            load_x(0)
            sp.dma_start(wq_nat, wqkv[0:D, :].rearrange("(m p) d -> p m d", p=P)).then_inc(w_in, 16)
            sp.dma_start(wvrk_nat[0:16, :], wqkv[D + HD:D + 2 * HD, :]).then_inc(w_in, 16)
            sp.dma_start(wvrk_nat[16:32, :], wrouter).then_inc(w_in, 16)
            sp.dma_start(wvrk_nat[32:48, :], wqkv[D:D + HD, :]).then_inc(w_in, 16)
            load_x(1)
            for m in range(KC):
                sp.dma_start(bq[:, m:m + 1], column(bqkv[m * P:(m + 1) * P])).then_inc(b_in, 16)
            sp.wait_ge(consts, 1)
            sp.dma_start(bvrk[0:16, :], column(bqkv[D + HD:D + 2 * HD])).then_inc(b_in, 16)
            sp.dma_start(bvrk[32:48, :], column(bqkv[D:D + HD])).then_inc(b_in, 16)
            sp.dma_start(wo_nat, wout.rearrange("(m p) d -> p m d", p=P)).then_inc(wo_in, 16)
            load_x(2)
            load_x(3)
            sp.dma_start(bo[:, :], bout.partition_broadcast(P)).then_inc(bo_in, 16)

            def load_k(start, stop):
                sp.wait_ge(k_stored, 32 * (stop // GW))
                for r in range(4):
                    sp.dma_start(k_all[16 * r:16 * r + 16, start:stop].bitcast(F32), k_d[r // 2, :, start:stop]
                                 ).then_inc(k_all_in, 16)

            def load_q(b, buf, half):
                hs = slice(half * H // 2, (half + 1) * H // 2)
                for r in range(4):
                    src = q_d[r % 2].rearrange("(h d) t -> d h t", d=HD)[:, hs, bass.ds(b * S, S)]
                    sp.dma_start(qs[16 * r:16 * r + 16, buf, hs, :].bitcast(F32), src).then_inc(q_in[buf][half], 16)

            sp.wait_ge(list_init, 1)
            sp.dma_start(slots_d.rearrange("(p j) a -> p (j a)", p=P),
                         slots[:, 0:MT, :].rearrange("p j a -> p (j a)")).then_inc(init_stored, 16)
            def store_xn(g):
                sp.wait_ge(xn_ready, GT * (g + 1))
                sp.dma_start(xn_d[g * GW:(g + 1) * GW, :].rearrange("(u p) d -> p u d", p=P), xn[:, g % 2]
                             ).then_inc(xn_stored[g % 2], 16)

            store_xn(0)
            for g in range(NG):
                cols = slice(g * GW, (g + 1) * GW)
                sp.wait_ge(kl_ready, g + 1)
                for a in range(2):
                    sp.dma_start(k_d[a, :, cols], khl[32:48, a, :].bitcast(F32)).then_inc(k_stored, 16)
                if g < NG - 1:
                    store_xn(g + 1)
                else:
                    for r in range(2):
                        sp.wait_ge(xn_stored[r], 16 * NG // 2)
                    sp.wait_ge(vrT_ps, NG)
                    sp.wait_ge(q_stored, 32)
                    for half in range(2):
                        load_q(0, 0, half)
                sp.wait_ge(ql_ready, KC * (g + 1))
                for a in range(2):
                    sp.dma_start(q_d[a, :, cols].rearrange("(m p) t -> p m t", p=P), qhl[:, a].bitcast(F32)
                                 ).then_inc(q_stored, 16)
                if g == 1:
                    load_k(0, GW)

            def load_m(b, buf):
                sp.wait_ge(mtl_ready, b + 1)
                for a in range(2):
                    sp.dma_start(qs[64 + a:65 + a, buf, :, :].bitcast(F32), mt[:, buf, a, :].bitcast(F32)).then_inc(m_in[buf], 16)

            def during(b, buf):
                sp.wait_ge(s_ps, b * 12 + 6)
                load_q(b + 2, buf, 0)
                load_m(b + 1, 1 - buf)
                sp.wait_ge(s_ps, b * 12 + 12)
                load_q(b + 2, buf, 1)

            load_k(GW, T)
            sp.wait_ge(q_stored, 32 * NG)
            sp.wait_ge(w_ps, 3)
            for half in range(2):
                load_q(1, 1, half)
            sp.wait_ge(qs_padded, 2)
            load_m(0, 0)
            with sp.Fori(0, B // 2 - 2) as i:
                for u in range(2):
                    during(i * 2 + u, u)
            for u in range(2):
                during(B - 4 + u, u)
            load_m(B - 1, 1)
            for b in range(2):
                sp.wait_ge(scattered[b], 16 * TOP_K * NT // 2)
            sp.dma_start(slots[:, 0:MT, :].rearrange("p j a -> p (j a)"),
                         slots_d.rearrange("(p j) a -> p (j a)", p=P)).then_inc(list_in, 16)

            for start, stop in ((0, (B - 1) * S), ((B - 1) * S, T)):
                sp.wait_ge(o_added, 2 * (stop // S))
                sp.dma_start(out_rows[start:stop, :].rearrange("(u p) d -> p u d", p=P),
                             xs[:, start // P:stop // P, :]).then_inc(base_stored, 16)
            sp.wait_ge(base_stored, 32)
            for r in range(RING):
                sp.wait_ge(y_sent[r], 16 * tiles_on(r))

        @block.gpsimd
        def _(pool):
            const = Steps(pool, masks)
            pool.memset(bvrk[:, :], 0.0).then_inc(consts, 1)
            pool.wait_ge(consts, 1)
            for t in (ident, ident_b):
                const(pool.memset(t[:, :], 0.0))
            for t in (ident, ident_b):
                const(pool.affine_select(out=t[:, :], in_=t[:, :], compare_op=ALU.not_equal, fill=1.0, base=0,
                                   pattern=[[-1, P]], channel_multiplier=1))
            const(pool.memset(mask_q[:], 0.0))
            const(pool.memset(mask_k[:], 0.0))
            const(pool.memset(below[:], 1.0))
            const(pool.affine_select(out=mask_q[:], in_=mask_q[:], compare_op=ALU.is_ge, fill=MASKED, base=0,
                               pattern=[[0, 2], [-1, P]], channel_multiplier=1))
            const(pool.affine_select(out=mask_k[:], in_=mask_k[:], compare_op=ALU.is_ge, fill=MASKED, base=0,
                               pattern=[[0, 4], [1, P]], channel_multiplier=-1))
            const(pool.affine_select(out=below[:], in_=below[:], compare_op=ALU.is_ge, fill=0.0, base=-1,
                               pattern=[[1, P]], channel_multiplier=-1))
            const(pool.memset(ones_b[:], 1.0))
            const(pool.memset(k_all[64:128].bitcast(F32), 0.0))
            const(pool.memset(ks[64:128].bitcast(F32), 0.0))
            const(pool.memset(v_all[:, :, HD + 1:VW], 0.0))
            const(pool.memset(v_all[:, :, HD:HD + 1], 1.0))
            const(pool.memset(ks[64:66].bitcast(F32), 1.0))
            const(pool.memset(scan_t[:], 0.0))
            const(pool.memset(scan_e[:], 0.0))
            const(pool.iota(iota_e[:], [[1, E]], base=0, channel_multiplier=0,
                      allow_small_or_imprecise_dtypes=True))
            const(pool.iota(row_coef[:, :, :, 0], [[P, NT], [0, TOP_K]], base=0, channel_multiplier=1))
            const(pool.iota(tile_no[:], [[1, MT]], base=0, channel_multiplier=0,
                      allow_small_or_imprecise_dtypes=True))
            pool.iota(slots[:], [[0, MT + RING], [-NOROW, 2]], base=NOROW, channel_multiplier=0
                      ).then_inc(list_init, 1)

            def add_bias(g):
                pool.wait_ge(bo_in, 16)
                pool.wait_ge(xn_ready, GT * (g + 1))
                for t in range(GT * g, GT * (g + 1)):
                    pool.tensor_tensor(xs[:, t, :], xs[:, t, :], bo[:, :], ALU.add).then_inc(xb_ready, 1)

            for g in range(NG):
                add_bias(g)

            def copy_kv(b, buf):
                if isinstance(b, int) and b < 2:
                    pool.wait_ge(k_all_in, 64)
                else:
                    pool.wait_ge(kv_ready, b * 2)
                pool.tensor_copy(ks[0:64, buf, :], k_all[0:64, bass.ds(b * S, S)]).then_inc(kv_ready, 1)
                pool.wait_ge(kv_ready, b * 2 + 1)
                pool.tensor_copy(vs[:, buf], v_all[:, bass.ds(b * 2, 2), :]).then_inc(kv_ready, 1)

            pool.wait_ge(vrT_ps, NG)
            for r in range(2):
                pool.wait_ge(xn_stored[r], 16 * NG // 2)
            pool.wait_ge(xb_ready, NT)
            pool.memset(qs[64:128, 0].bitcast(F32), 0.0).then_inc(qs_padded, 1)
            pool.wait_ge(qs_padded, 1)
            pool.wait_ge(vl_ready, NG)
            copy_kv(0, 0)
            pool.wait_ge(kv_ready, 2)
            pool.wait_ge(w_ps, 3)
            pool.wait_ge(q_stored, 32 * NG)
            pool.wait_ge(k_stored, 32 * NG)
            pool.memset(qs[64:128, 1].bitcast(F32), 0.0).then_inc(qs_padded, 1)
            pool.wait_ge(qs_padded, 2)
            copy_kv(1, 1)

            pool.wait_ge(kv_ready, 4)
            pool.wait_ge(init_stored, 16)
            last_slot = pool.to_reg(P * MT - 1)

            def after(sem, value):
                pool.wait_ge(sem, value)
                pool.sem_inc(pool_gate, 1)

            def scatter_slots(t, buf, used):
                if used is not None:
                    pool.wait_ge(scattered[buf], used)
                pool.tensor_copy(scat_to[:, buf, :], slot_i[:, bass.ds(t, 1), :]).then_inc(scat_copied, 1)
                pool.tensor_copy(scat_val[:, buf], row_coef[:, bass.ds(t, 1)].rearrange("p a k b -> p (a k) b")
                                 ).then_inc(scat_copied, 1)
                for k in range(TOP_K):
                    if k == 0:
                        after(scat_copied, t * 2 + 2)
                    pool.indirect_dma_start(
                        slots_d, bass.IndirectOffsetOnAxis(ap=scat_to[:, buf, k:k + 1], axis=0),
                        scat_val[:, buf, k, :], None, bounds_check=last_slot, oob_is_err=False,
                    ).then_inc(scattered[buf], 16)

            def next_kv(b, buf):
                pool.wait_ge(pv_ps, (b - 1) * NQ)
                copy_kv(b, buf)

            pool.wait_ge(k_all_in, 128)
            for u in range(2):
                next_kv(2 + u, u)
                pool.wait_ge(route_ready, 1)
                for t in range(4 * u, 4 * u + 4):
                    scatter_slots(t, t % 2, 16 * TOP_K * (t // 2) if t >= 2 else None)
            with pool.Fori(2, B // 2) as i:
                for u in range(2):
                    next_kv(i * 2 + u, u)
                    for v in range(2):
                        scatter_slots(i * 4 + (2 * u + v), v, (i * 2 + u) * (16 * TOP_K))
            assert NT == 8 + 4 * (B // 2 - 2)

            pool.wait_ge(kv_ready, 2 * B)
            pool.wait_ge(rows_ready, 1)
            last_row = pool.to_reg(T - 1)
            pool.wait_ge(s_ps, 12 * (B - 1))

            def gather(j, r, wait):
                if wait:
                    pool.wait_ge(xgT_ps, j - RING + 1)
                pool.tensor_copy(get_now[:, r:r + 1], get_row[:, bass.ds(j, 1)]).then_inc(now_ready, 1)
                after(now_ready, j + 1)
                pool.indirect_dma_start(
                    xg[:, r, :], None, xn_d, bass.IndirectOffsetOnAxis(ap=get_now[:, r:r + 1], axis=0),
                    bounds_check=last_row, oob_is_err=False).then_inc(gathered[r], 16)

            def send(j, r, before):
                pool.wait_ge(y_ready, j + 1)
                pool.tensor_copy(put_now[:, r:r + 1], slots[:, bass.ds(j, 1), 0]).then_inc(put_ready, 1)
                pool.wait_ge(put_ready, j + 1)
                if before is None:
                    after(base_stored, 32)
                else:
                    after(y_sent[(r - 1) % RING], before)
                pool.indirect_dma_start(
                    out_rows, bass.IndirectOffsetOnAxis(ap=put_now[:, r:r + 1], axis=0), ys[:, r, :], None,
                    bounds_check=last_row, oob_is_err=False, compute_op=ALU.add).then_inc(y_sent[r], 16)

            AHEAD = RING - 1

            def tiles(base, turn, first, n=RING):
                for u in range(n):
                    if n == RING:
                        gather(base + u + AHEAD, (u + AHEAD) % RING, not (first and u == 0))
                    if first and u == 2:
                        send(0, 0, None)
                    elif not (first and u < 2):
                        send(base + u - 2, (u - 2) % RING, turn * 16 + (16 if u == 3 else 0))

            assert REST == AHEAD
            for j in range(AHEAD):
                gather(j, j, False)
            tiles(0, 0, True)
            with pool.Fori(1, TURNS) as i:
                tiles(i * RING, i, False)
            tiles(TURNS * RING, TURNS, False, REST)
            for j in (MT - 2, MT - 1):
                send(j, j % RING, 16 * ((j - 1) // RING + 1))
            for r in range(RING):
                pool.wait_ge(gathered[r], 16 * tiles_on(r))

        @block.tensor
        def _(pe):
            pe.wait_ge(masks, 4)
            pe.wait_ge(w_in, 16 * N_W)
            for c in range(KC):
                for m in range(KC):
                    last = pe.transpose(bank[:, 6, c * D + m * P:c * D + (m + 1) * P],
                                        wq_nat[:, m, c * P:(c + 1) * P], ident[:, :])
            last.then_inc(w_ps, 1)
            for c in range(KC):
                last = pe.transpose(bank[:, 5, c * 48:(c + 1) * 48], wvrk_nat[0:48, c * P:(c + 1) * P],
                                    ident[0:48, 0:48])
            last.then_inc(w_ps, 1)
            def transpose_x(g):
                if g == 1:
                    pe.wait_ge(w_act, 2)
                    pe.wait_ge(w_dve, 2)
                for u in range(GT):
                    pe.wait_ge(xn_ready, GT * g + u + 1)
                    for c in range(KC):
                        t = pe.transpose(bank[:, XT_BANK[g % 2] + c, u * P:(u + 1) * P], xn[:, g % 2, u, c * P:(c + 1) * P],
                                         ident[:, :])
                        if u == GT - 1:
                            t.then_inc(xT_ps, 1)

            def project(g):
                pe.wait_ge(xT_act, 2 * g + 1)
                if g == 0:
                    pe.wait_ge(xT_dve, 1)
                if g:
                    pe.wait_ge(vr_ready, g)
                    pe.wait_ge(kl_ready, g)
                for c in range(KC):
                    mm = pe.matmul(bank[0:48, 2, :], wvrkT[:, c, :], xnT[:, g % 2, c, :],
                                   start=(c == 0), stop=(c == KC - 1))
                mm.then_inc(proj_ps, 1)
                if 0 < g < NG - 1:
                    transpose_x(g + 1)
                for m in range(KC):
                    if g:
                        pe.wait_ge(ql_ready, KC * (g - 1) + m + 1)
                    for c in range(KC):
                        mm = pe.matmul(bank[:, 3 + m, :], wqT[:, c, m * P:(m + 1) * P], xnT[:, g % 2, c, :],
                                       start=(c == 0), stop=(c == KC - 1))
                    mm.then_inc(proj_ps, 1)

            transpose_x(0)
            pe.wait_ge(wo_in, 16)
            for c in range(KC):
                for m in range(KC):
                    last = pe.transpose(bank[:, 7, c * D + m * P:c * D + (m + 1) * P],
                                        wo_nat[:, m, c * P:(c + 1) * P], ident[:, :])
            last.then_inc(w_ps, 1)
            pe.wait_ge(w_act, 2)
            for g in range(NG):
                project(g)
                if g == 0:
                    transpose_x(1)
                pe.wait_ge(vr_ready, g + 1)
                if g:
                    pe.wait_ge(vl_ready, g)
                for u in range(GT):
                    t = pe.transpose(bank[:, 5, u * 32:(u + 1) * 32], vr[0:32, u * P:(u + 1) * P],
                                     ident[0:32, 0:32])
                t.then_inc(vrT_ps, 1)

            def scores_for_max(b, buf, n):
                pair, qt = n // 2, n % 2
                if n == 0:
                    pe.wait_ge(q_in[buf][0], 64 * (b // 2 + 1) if isinstance(b, int) else (b - buf) * 32 + 64)
                if n == 8:
                    pe.wait_ge(q_in[buf][1], 64 * (b // 2 + 1) if isinstance(b, int) else (b - buf) * 32 + 64)
                banks = max_banks(b)
                if isinstance(b, int) and b == 0:
                    if n >= banks:
                        pe.wait_ge(max_done, n - banks + 1)
                elif n >= 2:
                    pe.wait_ge(max_done, b * 16 + (n - 1))
                elif not (isinstance(b, int) and b < 3):
                    pe.wait_ge(o_added, b * 2 - 5 + n)
                A = bank[:, n % banks, :]
                for k in range(2):
                    pe.matmul(A[:, k * S:(k + 1) * S], qs[:, buf, 2 * pair + k, qt * P:(qt + 1) * P],
                              k_all[:, bass.ds(b * S, S)], start=(k == 0), stop=True, skip_group_check=True)
                diag = A.rearrange("p (k t) -> p k t", k=2)[:, :, qt * P:(qt + 1) * P]
                pe.matmul(diag, ident_b[:, :], mask_q[:], start=False, stop=True,
                          skip_group_check=True).then_inc(p1_ps, 1)

            def transpose_max(b, buf):
                pe.wait_ge(max_done, b * 16 + 16)
                for qt in range(2):
                    t = pe.transpose(bank[0:H, 7, qt * P:(qt + 1) * P], nmax[:, buf, qt, :], ident[:, :])
                t.then_inc(mt_ps, 1)

            def scores(b, buf, q, r):
                n = 3 * q + r
                if not (isinstance(b, int) and b == 0 and n < 2):
                    pe.wait_ge(exp_done, b * 12 + (n - 1))
                A = bank[:, 2 + n % 2, :]
                if r < 2:
                    h0 = 4 * q + 2 * r
                    pe.matmul(A, ks[:, buf, 0:P], qs[:, buf, h0:h0 + 2, :], start=True, stop=True)
                    diag = A.rearrange("p (k t) -> p k t", k=2)[:, :, 0:P]
                    mm = pe.matmul(diag, ident_b[:, :], mask_k[:, 0:2, :], start=False, stop=True,
                                   skip_group_check=True)
                else:
                    pe.matmul(A, ks[:, buf, P:2 * P], qs[:, buf, 4 * q:4 * q + 4, P:2 * P],
                              start=True, stop=True)
                    mm = pe.matmul(A, ident_b[:, :], mask_k[:], start=False, stop=True, skip_group_check=True)
                mm.then_inc(s_ps, 1)

            def weigh_v(b, buf, q):
                pe.wait_ge(exp_done, b * 12 + (3 * q + 3))
                if not (isinstance(b, int) and b == 0 and q < 2):
                    pe.wait_ge(ct_ready, b * NQ + (q - 1))
                o = bank[:, 4 + q % 2, :]
                for j in range(4):
                    pe.matmul(o[32 * j:32 * j + 32, 0:S], vs[:, buf, 0, :],
                              pt[:, (3 * q + j // 2) % 6, (j % 2) * S:(j % 2 + 1) * S], start=True, stop=True)
                for j in range(4):
                    mm = pe.matmul(o[32 * j:32 * j + 32, P:S], vs[:, buf, 1, :],
                                   pt[:, (3 * q + 2) % 6, j * P:(j + 1) * P], start=False, stop=True,
                                   skip_group_check=True)
                mm.then_inc(pv_ps, 1)

            def context(b, buf, qt):
                if qt == 0:
                    pe.wait_ge(ct_ready, b * NQ + NQ)
                if isinstance(b, int) and b == 0 and qt == 0:
                    pe.wait_ge(route_ready, 1)
                else:
                    pe.wait_ge(ctx_ready, b * 2 + qt)
                for q in range(NQ):
                    t = pe.transpose(bank[:, 6, q * P:(q + 1) * P], ct[:, buf, q, qt * P:(qt + 1) * P],
                                     ident[:, :])
                t.then_inc(c_ps, 1)

            def transpose_context(b, qt):
                pe.wait_ge(ctx_ready, b * 2 + (qt + 1))
                for c in range(KC):
                    t = pe.transpose(bank[:, qt, c * P:(c + 1) * P], ctx_n[:, qt, c * P:(c + 1) * P], ident[:, :])
                t.then_inc(t_ps, 1)

            def project_out(b, qt):
                pe.wait_ge(cxt_ready, b * 2 + (qt + 1))
                for c in range(KC):
                    mm = pe.matmul(bank[:, qt, 0:D], cxt[:, qt, c, :], woT[:, c, :], start=(c == 0),
                                   stop=(c == KC - 1))
                mm.then_inc(o_ps, 1)

            def batch(b, buf, first=False, ahead=True):
                other = 1 - buf
                for s in range(12):
                    if ahead and s < 8:
                        scores_for_max(b + 1, other, 2 * s)
                    if s == 0:
                        pe.wait_ge(m_in[buf], 32 * (b // 2 + 1) if isinstance(b, int) else (b - buf) * 16 + 32)
                        pe.wait_ge(kv_ready, b * 2 + 2)
                    scores(b, buf, s // 3, s % 3)
                    if ahead and s < 8:
                        scores_for_max(b + 1, other, 2 * s + 1)
                    if s == 8 and ahead:
                        transpose_max(b + 1, other)
                    if s == 0 and not first:
                        weigh_v(b - 1, other, NQ - 1)
                    if s in (4, 7, 10):
                        weigh_v(b, buf, s // 3 - 1)
                    if not first:
                        if s == 2:
                            context(b - 1, other, 0)
                        if s == 6:
                            context(b - 1, other, 1)
                        if s in (8, 9):
                            transpose_context(b - 1, s - 8)
                        if s in (10, 11):
                            project_out(b - 1, s - 10)

            def count_choices():
                pe.wait_ge(masks, 11)
                pe.wait_ge(xT_act, 2 * NG - 1)
                pe.wait_ge(chosen_ready, len(CHOICE_PARTS))
                flat = chosen[:].rearrange("p t e -> p (t e)")
                pe.matmul(bank[:, 6, 0:NT * E], below[:, :], flat, start=True, stop=True)
                pe.matmul(bank[:, 6, NT * E:2 * NT * E], ones_b[:, :], flat, start=True, stop=True).then_inc(place_ps, 1)

            pe.wait_ge(masks, 16)
            pe.wait_ge(qs_padded, 1)
            pe.wait_ge(k_all_in, 64)
            pe.wait_ge(vl_ready, NG)
            pe.wait_ge(ql_ready, KC * NG)
            for n in range(16):
                scores_for_max(0, 0, n)
                if n == max_banks(0) - 1:
                    count_choices()
            pe.wait_ge(xT_act, 2 * NG - 1)
            transpose_max(0, 0)
            pe.wait_ge(qs_padded, 2)
            batch(0, 0, first=True)
            pe.wait_ge(k_all_in, 128)
            batch(1, 1)
            with pe.Fori(1, B // 2 - 1) as i:
                batch(i * 2, 0)
                batch(i * 2 + 1, 1)
            batch(B - 2, 0)
            batch(B - 1, 1, ahead=False)

            pe.wait_ge(experts_in, 16 * N_EXP)
            pe.wait_ge(tile_e_ready, 1)

            def tile_xT(j, r, came):
                pe.wait_ge(gathered[r], came)
                for c in range(KC):
                    t = pe.transpose(bank[:, 7, c * P:(c + 1) * P], xg[:, r, c * P:(c + 1) * P], ident[:, :])
                t.then_inc(xgT_ps, 1)

            def expert(j):
                return pe.value_load(tile_e[0:1, bass.ds(j, 1)], min_val=0, max_val=E - 1)

            def tile_gate_up(j, buf, e):
                pe.wait_ge(xgT_ready, j + 1)
                for c in range(KC):
                    mm = pe.matmul(bank[:, 2 + buf, :], xT[:, buf, c, :],
                                   wgu[:, bass.ds(e * KC + c, 1), :], start=(c == 0), stop=(c == KC - 1))
                mm.then_inc(gu_ps, 1)

            def tile_hT(j, buf):
                pe.wait_ge(h_ready, j + 1)
                for c in range(FC):
                    t = pe.transpose(bank[:, 6, c * P:(c + 1) * P], hh[:, buf, c * P:(c + 1) * P], ident[:, :])
                t.then_inc(hT_ps, 1)

            def tile_down(j, buf, e):
                pe.wait_ge(hT_ready, j + 1)
                for c in range(FC):
                    mm = pe.matmul(bank[:, 4 + buf, 0:D], hT[:, buf, c, :],
                                   wdn[:, bass.ds(e * FC + c, 1), :], start=(c == 0), stop=(c == FC - 1))
                mm.then_inc(dn_ps, 1)

            def tiles(base, turn, first, n=RING):
                es = {}
                for u in range(n):
                    j = base + u
                    es[u] = expert(j)
                    tile_gate_up(j, u % 2, es[u])
                    if not (first and u < 2) and u < 2:
                        es[u - 2] = expert(j - 2)
                    if not (n == REST and u == n - 1):
                        tile_xT(j + 1, (u + 1) % RING, turn * 16 + (32 if u == RING - 1 else 16))
                    if not (first and u < 2):
                        tile_down(j - 2, u % 2, es[u - 2])
                    if first:
                        last_output(u)
                    if not (first and u == 0):
                        tile_hT(j - 1, (u + 1) % 2)

            def last_output(u):
                if u == 0:
                    context(B - 1, 1, 0)
                if u == 1:
                    transpose_context(B - 1, 0)
                    context(B - 1, 1, 1)
                    project_out(B - 1, 0)
                    pe.wait_ge(ctx_ready, 2 * B)
                if u == 2:
                    transpose_context(B - 1, 1)
                    project_out(B - 1, 1)

            tile_xT(0, 0, 16)
            weigh_v(B - 1, 1, NQ - 1)
            tiles(0, 0, True)
            with pe.Fori(1, TURNS) as i:
                tiles(i * RING, i, False)
            tiles(TURNS * RING, TURNS, False, REST)
            e0, e1 = expert(MT - 2), expert(MT - 1)
            pe.wait_ge(y_ready, MT - 3)
            tile_down(MT - 2, MT % 2, e0)
            tile_hT(MT - 1, (MT - 1) % 2)
            pe.wait_ge(y_ready, MT - 2)
            tile_down(MT - 1, (MT - 1) % 2, e1)

        @block.scalar
        def _(act):
            def root(g):
                ts = slice(g * GT, (g + 1) * GT)
                act.wait_ge(var_ready, g + 1)
                act.activation(std0[:, ts], var_e[:, ts], ACT.Sqrt).then_inc(std_ready, 1)

            root(0)
            act.wait_ge(w_ps, 2)
            act.activation(wqT[:].rearrange("p c e -> p (c e)"), bank[:, 6, :], ACT.Copy,
                           scale=QSCALE).then_inc(w_act, 1)
            act.activation(wvrkT[:].rearrange("p c e -> p (c e)"), bank[:, 5, 0:KC * 48],
                           ACT.Copy).then_inc(w_act, 1)

            def exp_logits(part):
                start, stop = CHOICE_PARTS[part]
                act.wait_ge(shifted, part + 1)
                act.activation(probs[:, start * GT:stop * GT], logits[:, start * GT:stop * GT], ACT.Exp
                               ).then_inc(exped, 1)

            def keep_xT(g):
                act.wait_ge(xT_ps, 2 * g + 1)
                if g >= 2:
                    act.wait_ge(proj_ps, 3 * (g - 1))
                act.activation(xnT[:, g % 2, 0, :], bank[:, XT_BANK[g % 2], :], ACT.Copy).then_inc(xT_act, 1)
                if g:
                    act.wait_ge(xT_ps, 2 * g + 2)
                    act.activation(xnT[:, g % 2, 1, :], bank[:, XT_BANK[g % 2] + 1, :], ACT.Copy).then_inc(xT_act, 1)

            keep_xT(0)
            root(1)
            act.wait_ge(masks, 15)
            act.wait_ge(b_in, 64)
            for g in range(NG):
                act.wait_ge(proj_ps, 3 * g + 1)
                if g:
                    act.wait_ge(vrT_ps, g)
                act.activation(vr[0:32, :], bank[0:32, 2, :], ACT.Identity, bias=bvrk[0:32, :]
                               ).then_inc(vr_ready, 1)
                if g:
                    act.wait_ge(k_stored, 32 * g)
                act.activation(khl[32:48, 0, :], bank[32:48, 2, :], ACT.Identity, bias=bvrk[32:48, :]
                               ).then_inc(kh_ready, 1)
                if 0 < g < NG - 1:
                    keep_xT(g + 1)
                if g == 1:
                    root(3)
                if g == 2:
                    exp_logits(0)
                if g == 3:
                    exp_logits(1)
                if g:
                    act.wait_ge(q_stored, 32 * g)
                else:
                    act.wait_ge(w_ps, 2)
                    act.wait_ge(w_dve, 1)
                for m in range(KC):
                    act.wait_ge(proj_ps, 3 * g + 2 + m)
                    act.activation(qhl[:, 0, m, :], bank[:, 3 + m, :], ACT.Identity, bias=bq_s[:, m:m + 1]
                                   ).then_inc(qh_ready, 1)
                if g == 0:
                    keep_xT(1)
                    root(2)
                act.wait_ge(vrT_ps, g + 1)
                vl = bank[:, 5, 0:GT * 32].rearrange("p (u c) -> p u c", u=GT)
                act.activation(v_all[:, g * GT:(g + 1) * GT, 0:HD], vl[:, :, 0:HD], ACT.Copy)
                act.activation(logits[:, g * GT:(g + 1) * GT, :], vl[:, :, HD:HD + E], ACT.Copy
                               ).then_inc(vl_ready, 1)

            exp_logits(2)

            def exp_scores(b, n):
                act.wait_ge(s_ps, b * 12 + (n + 1))
                if not (isinstance(b, int) and b == 0 and n < 6):
                    act.wait_ge(pv_ps, b * NQ + (n // 3 - 1))
                act.activation(pt[:, n % 6, :], bank[:, 2 + n % 2, :], ACT.Exp).then_inc(exp_done, 1)

            def keep_context(b, buf, q):
                act.wait_ge(pv_ps, b * NQ + (q + 1))
                if not (isinstance(b, int) and b < 2):
                    act.wait_ge(c_ps, b * 2 - 2)
                act.activation(ct[:, buf, q, :], bank[:, 4 + q % 2, 0:S], ACT.Copy).then_inc(ct_ready, 1)

            def keep_cxt(b, qt):
                act.wait_ge(t_ps, b * 2 + (qt + 1))
                act.activation(cxt[:, qt].rearrange("p c t -> p (c t)"), bank[:, qt, 0:D], ACT.Copy
                               ).then_inc(cxt_ready, 1)

            def keep_max(b, buf):
                act.wait_ge(mt_ps, b + 1)
                act.activation(mt[:, buf, 0, :], bank[0:H, 7, 0:S], ACT.Copy).then_inc(mth_ready, 1)

            def load_experts(b, which):
                src = (wgate, wup, wdown)[which][bass.ds(b * (E // B), E // B)].rearrange("e (c p) f -> p (e c) f", p=P)
                rows = bass.ds(b * (E // B * KC), E // B * KC)
                dst = wdn[:, rows, :] if which == 2 else wgu[:, rows, which * F:(which + 1) * F]
                act.dma_start(dst, src).then_inc(experts_in, 16)

            def batch(b, buf, first=False, ahead=True):
                other = 1 - buf
                for s in range(12):
                    exp_scores(b, s)
                    if s in (3, 5, 7):
                        load_experts(b, s // 2 - 1)
                    if s == 0 and not first:
                        keep_context(b - 1, other, NQ - 1)
                    if s in (4, 7, 10):
                        keep_context(b, buf, s // 3 - 1)
                    if s == 8 and ahead:
                        keep_max(b + 1, other)
                    if s in (9, 10) and not first:
                        keep_cxt(b - 1, s - 9)

            keep_max(0, 0)
            batch(0, 0, first=True)
            batch(1, 1)
            with act.Fori(1, B // 2 - 1) as i:
                batch(i * 2, 0)
                batch(i * 2 + 1, 1)
            batch(B - 2, 0)
            batch(B - 1, 1, ahead=False)
            def tile_silu(j, buf):
                act.wait_ge(gu_ps, j + 1)
                act.activation(sg[:, buf, :], bank[:, 2 + buf, 0:F], ACT.Silu).then_inc(silu_ready, 1)

            def tile_xT(j, buf):
                act.wait_ge(xgT_ps, j + 1)
                act.activation(xT[:, buf].rearrange("p c t -> p (c t)"), bank[:, 7, 0:D], ACT.Copy
                               ).then_inc(xgT_ready, 1)

            def tile_y(j, r, sent):
                act.wait_ge(dn_ps, j + 1)
                if sent is not None:
                    act.wait_ge(y_sent[r], sent)
                act.activation(ys[:, r, :], bank[:, 4 + r % 2, 0:D], ACT.Copy).then_inc(y_ready, 1)

            def tiles(base, turn, first, n=RING):
                for u in range(n):
                    j = base + u
                    tile_silu(j, u % 2)
                    if not (n == REST and u == n - 1):
                        tile_xT(j + 1, (u + 1) % 2)
                    if first and 1 <= u < 3:
                        keep_cxt(B - 1, u - 1)
                    if u < 2 and not first:
                        tile_y(j - 2, u + 2, None if isinstance(turn, int) and turn == 1 else turn * 16 - 16)
                    elif u >= 2:
                        tile_y(j - 2, u - 2, None if first else turn * 16)

            tile_xT(0, 0)
            keep_context(B - 1, 1, NQ - 1)
            tiles(0, 0, True)
            tiles(RING, 1, False)
            with act.Fori(2, TURNS) as i:
                tiles(i * RING, i, False)
            tiles(TURNS * RING, TURNS, False, REST)
            for j in (MT - 2, MT - 1):
                tile_y(j, j % RING, 16 * (j // RING))

        @block.vector
        def _(dve):
            ln = Steps(dve, dve_ln)

            def normalise(g):
                ts = slice(g * GT, (g + 1) * GT)
                for t in range(ts.start, ts.stop):
                    dve.wait_ge(x_in[g], 16)
                    last = dve.bn_stats(stats[:, t, :], xs[:, t, :])
                ln(last)
                for t in range(ts.start, ts.stop):
                    last = dve.bn_aggr(mv[:, t, :], stats[:, t, :])
                ln(last)
                dve.tensor_scalar(var_e[:, ts], mv[:, ts, 1], LN_EPS, None, ALU.add).then_inc(var_ready, 1)
                dve.wait_ge(std_ready, g + 1)
                ln(dve.reciprocal(rstd[:, ts], std0[:, ts]))
                ln(dve.tensor_tensor(rstd[:, ts], rstd[:, ts], var_e[:, ts], ALU.mult))
                ln(dve.tensor_tensor(rstd[:, ts], rstd[:, ts], std0[:, ts], ALU.add))
                ln(dve.tensor_scalar(rstd[:, ts], rstd[:, ts], 0.5, None, ALU.mult))
                ln(dve.reciprocal(rstd[:, ts], rstd[:, ts]))
                if g >= 2:
                    dve.wait_ge(xT_ps, 2 * (g - 1))
                    dve.wait_ge(xn_stored[g % 2], 16 * (g // 2))
                for u in range(GT):
                    t = g * GT + u
                    dve.tensor_scalar(xn[:, g % 2, u, :], xs[:, t, :], mv[:, t, 0:1], rstd[:, t:t + 1],
                                      ALU.subtract, ALU.mult).then_inc(xn_ready, 1)


            normalise(0)
            dve.wait_ge(xT_ps, 2)
            dve.tensor_copy(xnT[:, 0, 1, :], bank[:, XT_BANK[0] + 1, :]).then_inc(xT_dve, 1)
            dve.wait_ge(b_in, 64)
            dve.tensor_scalar(bq_s[:, :], bq[:, :], QSCALE, None, ALU.mult).then_inc(w_dve, 1)
            dve.wait_ge(w_ps, 3)
            dve.tensor_copy(woT[:].rearrange("p c e -> p (c e)"), bank[:, 7, :]).then_inc(w_dve, 1)
            dve.wait_ge(w_dve, 2)
            normalise(1)
            rt = Steps(dve, dve_rt)
            choice = onehot.rearrange("p t k e -> p (t k) e")

            def choose(part):
                start, stop = CHOICE_PARTS[part]
                ts = slice(start * GT, stop * GT)

                def spread(ap, n):
                    return ap.unsqueeze(2).to_broadcast([P, (stop - start) * GT, n])

                dve.wait_ge(vl_ready, stop)
                rt(dve.tensor_reduce(rowstat[:, ts], logits[:, ts], AX.X, ALU.max))
                dve.tensor_tensor(logits[:, ts], logits[:, ts], spread(rowstat[:, ts], E), ALU.subtract
                                  ).then_inc(shifted, 1)
                dve.wait_ge(exped, part + 1)
                rt(dve.tensor_reduce(rowstat[:, ts], probs[:, ts], AX.X, ALU.add))
                rt(dve.reciprocal(rowstat[:, ts], rowstat[:, ts]))
                rt(dve.tensor_tensor(probs[:, ts], probs[:, ts], spread(rowstat[:, ts], E), ALU.mult))
                for t in range(ts.start, ts.stop):
                    last = dve.max(top_w[:, t, :], probs[:, t, :])
                rt(last)
                for t in range(ts.start, ts.stop):
                    last = dve.max_index(top_e[:, t, :], top_w[:, t, :], probs[:, t, :])
                rt(last)
                dve.wait_ge(masks, 21)
                rt(dve.tensor_reduce(rowstat[:, ts], top_w[:, ts, 0:TOP_K], AX.X, ALU.add))
                rt(dve.reciprocal(rowstat[:, ts], rowstat[:, ts]))
                rt(dve.tensor_tensor(row_coef[:, ts, :, 1].bitcast(F32), top_w[:, ts, 0:TOP_K],
                                     spread(rowstat[:, ts], TOP_K), ALU.mult))
                rt(dve.tensor_copy(top_ef[:, ts], top_e[:, ts, 0:TOP_K]))
                n = (stop - start) * GT * TOP_K
                rt(dve.tensor_tensor(choice[:, start * GT * TOP_K:stop * GT * TOP_K],
                                     top_ef[:, ts].rearrange("p t k -> p (t k)").unsqueeze(2).to_broadcast([P, n, E]),
                                     iota_e[:].unsqueeze(1).to_broadcast([P, n, E]), ALU.is_equal))
                with nc.allow_low_precision(reason="each sum is 0 or 1"):
                    dve.tensor_reduce(chosen[:, ts], onehot[:, ts].rearrange("p t k e -> p t e k"), AX.X, ALU.add
                                      ).then_inc(chosen_ready, 1)

            for g in range(NG):
                dve.wait_ge(kh_ready, g + 1)
                dve.scalar_tensor_tensor(out=khl[32:48, 1, :], in0=bank[32:48, 2, :], scalar=bvrk[32:48, :],
                                         in1=khl[32:48, 0, :].bitcast(F32), op0=ALU.add, op1=ALU.subtract
                                         ).then_inc(kl_ready, 1)
                if g == 1:
                    normalise(3)
                if g == 2:
                    choose(0)
                if g == 3:
                    choose(1)
                for m in range(KC):
                    dve.wait_ge(qh_ready, KC * g + m + 1)
                    dve.scalar_tensor_tensor(out=qhl[:, 1, m, :], in0=bank[:, 3 + m, :],
                                             scalar=bq_s[:, m:m + 1], in1=qhl[:, 0, m, :].bitcast(F32),
                                             op0=ALU.add, op1=ALU.subtract).then_inc(ql_ready, 1)
                if g == 0:
                    normalise(2)

            choose(2)

            scanned_t = scan_t[:, (NT.bit_length() - 1) % 2]
            scanned_e = scan_e[:, (E.bit_length() - 1) % 2]
            count = scanned_t[:, PADT + NT - 1, :]
            before = scanned_t[:, PADT - 1:PADT + NT - 1, :]
            end = scanned_e[:, PADE:]

            def sum_over_tiles():
                dve.wait_ge(place_ps, 1)
                rt(dve.tensor_copy(scan_t[:, 0, PADT:, :], bank[:, 6, NT * E:2 * NT * E].rearrange("p (t e) -> p t e", t=NT)))
                src, step = 0, 1
                while step < NT:
                    rt(dve.tensor_tensor(scan_t[:, 1 - src, PADT:, :], scan_t[:, src, PADT:, :],
                                         scan_t[:, src, PADT - step:PADT + NT - step, :], ALU.add))
                    src, step = 1 - src, 2 * step

            def first_rows():
                rt(dve.tensor_scalar(ntile_i[:, :], count, float(P - 1), None, ALU.add))
                rt(dve.tensor_scalar(ntile_i[:, :], ntile_i[:, :], P.bit_length() - 1, None,
                                     ALU.logical_shift_right))
                rt(dve.tensor_copy(scan_e[:, 0, PADE:], ntile_i[:, :]))
                esrc, step = 0, 1
                while step < E:
                    rt(dve.tensor_tensor(scan_e[:, 1 - esrc, PADE:], scan_e[:, esrc, PADE:],
                                         scan_e[:, esrc, PADE - step:PADE + E - step], ALU.add))
                    esrc, step = 1 - esrc, 2 * step
                rt(dve.tensor_tensor(first_row[:, :], end, ntile_i[:, :], ALU.subtract))
                rt(dve.tensor_scalar(first_row[:, :], first_row[:, :], float(P), None, ALU.mult))

            def choice_slots():
                rt(dve.tensor_tensor(probs[:], before, bank[:, 6, 0:NT * E].rearrange("p (t e) -> p t e", t=NT),
                                     ALU.add))
                rt(dve.tensor_tensor(probs[:], probs[:], first_row[:].unsqueeze(1).to_broadcast([P, NT, E]),
                                     ALU.add))
                for k in range(TOP_K):
                    last = dve.tensor_tensor(onehot[:, :, k, :], onehot[:, :, k, :], probs[:], ALU.mult)
                rt(last)
                rt(dve.tensor_reduce(slot_f[:].rearrange("p t k -> p (t k)"), choice, AX.X, ALU.add))

            def slot_numbers():
                rt(dve.tensor_copy(slot_i[:], slot_f[:]))
                rt(dve.tensor_scalar(slot_p[:], slot_i[:], P - 1, None, ALU.bitwise_and))
                rt(dve.tensor_scalar(slot_i[:], slot_i[:], P.bit_length() - 1, None, ALU.logical_shift_right))
                rt(dve.tensor_copy(slot_pf[:], slot_p[:]))
                rt(dve.tensor_copy(slot_f[:], slot_i[:]))
                rt(dve.scalar_tensor_tensor(out=slot_f[:], in0=slot_pf[:], scalar=float(MT), in1=slot_f[:],
                                            op0=ALU.mult, op1=ALU.add))
                dve.tensor_copy(slot_i[:], slot_f[:]).then_inc(route_ready, 1)

            def tile_experts():
                rt(dve.tensor_tensor(tile_ge, tile_no[:].unsqueeze(2).to_broadcast([1, MT, E]),
                                     end[0:1].unsqueeze(1).to_broadcast([1, MT, E]), ALU.is_ge))
                rt(dve.tensor_reduce(tile_ef[:], tile_ge, AX.X, ALU.add))
                dve.tensor_scalar(tile_e[:], tile_ef[:], float(E - 1), None, ALU.min).then_inc(tile_e_ready, 1)

            def row_max(b, buf, n):
                pair, qt = n // 2, n % 2
                dve.wait_ge(p1_ps, b * 16 + (n + 1))
                A = bank[:, n % max_banks(b), :].rearrange("p (k t) -> p k t", k=2)
                dve.tensor_reduce(nmax[:, buf, qt, 2 * pair:2 * pair + 2], A[:, :, 0:(qt + 1) * P], AX.X, ALU.max,
                                  negate=True).then_inc(max_done, 1)

            def split_max(b, buf):
                dve.wait_ge(mth_ready, b + 1)
                dve.tensor_tensor(mt[:, buf, 1, :], bank[0:H, 7, 0:S], mt[:, buf, 0, :].bitcast(F32),
                                  ALU.subtract).then_inc(mtl_ready, 1)

            def normalise_context(b, qt):
                dve.wait_ge(c_ps, b * 2 + (qt + 1))
                c = bank[:, 6, :].rearrange("p (h v) -> p h v", h=H)
                dve.reciprocal(rden[:, qt, :], c[:, :, HD]).then_inc(rden_ready, 1)
                dve.wait_ge(rden_ready, b * 2 + (qt + 1))
                dve.tensor_tensor(ctx_n[:, qt].rearrange("p (h v) -> p h v", h=H), c[:, :, 0:HD],
                                  rden[:, qt, :].unsqueeze(2).to_broadcast([P, H, HD]), ALU.mult
                                  ).then_inc(ctx_ready, 1)

            def add_out(b, qt):
                dve.wait_ge(o_ps, b * 2 + (qt + 1))
                tile = xs[:, bass.ds(b * 2 + qt, 1), :].rearrange("p a d -> p (a d)")
                dve.tensor_tensor(tile, tile, bank[:, qt, 0:D], ALU.add).then_inc(o_added, 1)

            def batch(b, buf, first=False, ahead=True):
                other = 1 - buf
                for s in range(8):
                    if ahead:
                        row_max(b + 1, other, 2 * s)
                        row_max(b + 1, other, 2 * s + 1)
                    if s in (3, 7) and not first:
                        normalise_context(b - 1, s // 4)
                    if s == 1 and first:
                        first_rows()
                    if not ahead and s == 4:
                        dve.wait_ge(list_in, 16)
                        dve.tensor_scalar(get_row[:, :], slots[:, :, 0], T - 1, None, ALU.bitwise_and
                                          ).then_inc(rows_ready, 1)
                    if isinstance(b, int) and b == 1 and s == 0:
                        slot_numbers()
                if ahead:
                    split_max(b + 1, other)
                if first:
                    choice_slots()
                else:
                    for qt in range(2):
                        add_out(b - 1, qt)

            for n in range(16):
                row_max(0, 0, n)
            split_max(0, 0)
            sum_over_tiles()
            dve.wait_ge(xb_ready, NT)
            batch(0, 0, first=True)
            batch(1, 1)
            with dve.Fori(1, B // 2 - 1) as i:
                batch(i * 2, 0)
                batch(i * 2 + 1, 1)
            batch(B - 2, 0)
            tile_experts()
            batch(B - 1, 1, ahead=False)

            def tile_h(j, buf):
                dve.wait_ge(silu_ready, j + 1)
                dve.scalar_tensor_tensor(out=hh[:, buf, :], in0=sg[:, buf, :],
                                         scalar=slots[:, bass.ds(j, 1), 1].bitcast(F32),
                                         in1=bank[:, 2 + buf, F:2 * F], op0=ALU.mult, op1=ALU.mult
                                         ).then_inc(h_ready, 1)

            def tile_hT(j, buf):
                dve.wait_ge(hT_ps, j + 1)
                dve.tensor_copy(hT[:, buf].rearrange("p c t -> p (c t)"), bank[:, 6, 0:F]).then_inc(hT_ready, 1)

            def tiles(base, first, n=RING):
                for u in range(n):
                    tile_h(base + u, u % 2)
                    if first:
                        if u < 2:
                            normalise_context(B - 1, u)
                        if 1 <= u < 3:
                            add_out(B - 1, u - 1)
                    if not (first and u == 0):
                        tile_hT(base + u - 1, (u + 1) % 2)

            tiles(0, True)
            with dve.Fori(1, TURNS) as i:
                tiles(i * RING, False)
            tiles(TURNS * RING, False, REST)
            tile_hT(MT - 1, (MT - 1) % 2)


_INS = ['L0_attn_x', 'L0_attn_Wqkv_w', 'L0_attn_Wqkv_b', 'L0_attn_out_w', 'L0_attn_out_b',
        'L0_ffn_w_router', 'L0_ffn_w_gate', 'L0_ffn_w_up', 'L0_ffn_w_down']
_OUTS = [((8, 256, 256), 'float32')]


def kernel(**inputs):
    import numpy as _np
    import concourse.bacc as _bacc
    from concourse import mybir as _mybir
    from concourse.bass_utils import run_bass_kernel_spmd as _run

    nc = _bacc.Bacc("TRN2", target_bir_lowering=False, num_devices=1)
    arrays, args = {}, []
    for name in _INS:
        a = _np.ascontiguousarray(inputs[name])
        arrays[f"in_{name}_dram"] = a
        args.append(nc.dram_tensor(f"in_{name}_dram", a.shape, _mybir.dt.from_np(a.dtype), kind="ExternalInput").ap())
    for i, (shape, dtype) in enumerate(_OUTS):
        dt = _mybir.dt.from_np(_np.dtype(dtype))
        args.append(nc.dram_tensor(f"out_{i}_dram", shape, dt, kind="ExternalOutput").ap())
    attention_and_experts(nc, *args)
    r = _run(nc, [arrays], core_ids=[0])
    return r.results[0]["out_0_dram"]
```
